# Optimizing a Trainium2 kernel written in Bass

```python
import numpy as np
import jax
import jax.numpy as jnp

def _softmax(x, axis=-1):
    return jax.nn.softmax(x, axis=axis)

def _gelu(x):
    return jax.nn.gelu(x, approximate=True)

def _silu(x):
    return jax.nn.silu(x)

def _sigmoid(x):
    return jax.nn.sigmoid(x)

def _layernorm(x, axis=-1, eps=1e-05):
    m = jnp.mean(x, axis=axis, keepdims=True)
    v = jnp.var(x, axis=axis, keepdims=True)
    return (x - m) / jnp.sqrt(v + eps)

def _scatter_add(tgt, idx, src, axis=0):
    return tgt.at[idx].add(src)

def _segment_sum(src, seg, n):
    return jax.ops.segment_sum(src, seg, n)
kernel_name = 'mk_sandwich_d1_jaxref_r4_922294'

def setup_inputs(seed: int=0):
    np.random.seed(seed)
    _w = jnp.asarray

    def _L0_attn_setup():
        import jax, jax.numpy as jnp
        import numpy as np
        IMG_SIZE = 224
        PATCH_SIZE = 16
        CONTEXT_LEN = 79
        LATENT_DIM = 256
        NUM_HEADS = 16
        NUM_PATCHES = (IMG_SIZE // PATCH_SIZE) ** 2
        SEQ_LEN = NUM_PATCHES + CONTEXT_LEN
        BATCH = 8

        def prefix_lm_mask(num_img_patches, total):
            m = np.tril(np.ones((total, total), dtype=np.float32))
            m[:num_img_patches, :num_img_patches] = 1.0
            return jnp.asarray(m)
        key = jax.random.key(seed)
        k_x, k_q, k_k, k_v, k_o, k_b = jax.random.split(key, 6)
        d = LATENT_DIM
        scale = 1.0 / np.sqrt(d)
        return {'x': jax.random.normal(k_x, (BATCH, SEQ_LEN, d), dtype=jnp.float32), 'w_q': jax.random.normal(k_q, (d, d), dtype=jnp.float32) * scale, 'w_k': jax.random.normal(k_k, (d, d), dtype=jnp.float32) * scale, 'w_v': jax.random.normal(k_v, (d, d), dtype=jnp.float32) * scale, 'w_o': jax.random.normal(k_o, (d, d), dtype=jnp.float32) * scale, 'b_o': jax.random.normal(k_b, (d,), dtype=jnp.float32) * 0.01}
    _L0_attn_in = _L0_attn_setup()

    def _L0_ffn_setup():
        import jax, jax.numpy as jnp
        import numpy as np
        E = 8
        TOP_K = 2
        ROUTE_SCALE = 1.0
        ALPHA = 1.702
        LIMIT = 7.0
        D = 256
        F = 256
        B, S = (2, 256)

        def swiglu(h):
            g = jnp.minimum(h[..., ::2], LIMIT)
            l = jnp.clip(h[..., 1::2], -LIMIT, LIMIT)
            return g * jax.nn.sigmoid(ALPHA * g) * (l + 1.0)
        if __name__ == '__main__':
            out = reference(**setup_inputs())
            print(out.shape, out.dtype)
        key = jax.random.key(seed)
        ks = jax.random.split(key, 16)
        sd = 1.0 / np.sqrt(D)
        sf = 1.0 / np.sqrt(F)
        return {'x': jax.random.normal(ks[0], (B, S, D), jnp.float32), 'gate_w': jax.random.normal(ks[1], (E, D), jnp.float32) * sd, 'gate_b': jax.random.normal(ks[2], (E,), jnp.float32) * 0.01, 'w1': jax.random.normal(ks[3], (E, 2 * F, D), jnp.float32) * sd, 'b1': jax.random.normal(ks[4], (E, 2 * F), jnp.float32) * 0.01, 'w3': jax.random.normal(ks[5], (E, 2 * F, D), jnp.float32) * sd, 'b3': jax.random.normal(ks[6], (E, 2 * F), jnp.float32) * 0.01, 'w2': jax.random.normal(ks[7], (E, D, F), jnp.float32) * sf, 'b2': jax.random.normal(ks[8], (E, D), jnp.float32) * 0.01, 'sw1': jax.random.normal(ks[9], (2 * F, D), jnp.float32) * sd, 'sb1': jax.random.normal(ks[10], (2 * F,), jnp.float32) * 0.01, 'sw3': jax.random.normal(ks[11], (2 * F, D), jnp.float32) * sd, 'sb3': jax.random.normal(ks[12], (2 * F,), jnp.float32) * 0.01, 'sw2': jax.random.normal(ks[13], (D, F), jnp.float32) * sf, 'sb2': jax.random.normal(ks[14], (D,), jnp.float32) * 0.01}
    _L0_ffn_in = _L0_ffn_setup()
    _d = {'L0_attn_x': _L0_attn_in['x'], 'L0_attn_w_q': _L0_attn_in['w_q'], 'L0_attn_w_k': _L0_attn_in['w_k'], 'L0_attn_w_v': _L0_attn_in['w_v'], 'L0_attn_w_o': _L0_attn_in['w_o'], 'L0_attn_b_o': _L0_attn_in['b_o'], 'L0_ffn_gate_w': _L0_ffn_in['gate_w'], 'L0_ffn_gate_b': _L0_ffn_in['gate_b'], 'L0_ffn_w1': _L0_ffn_in['w1'], 'L0_ffn_b1': _L0_ffn_in['b1'], 'L0_ffn_w3': _L0_ffn_in['w3'], 'L0_ffn_b3': _L0_ffn_in['b3'], 'L0_ffn_w2': _L0_ffn_in['w2'], 'L0_ffn_b2': _L0_ffn_in['b2'], 'L0_ffn_sw1': _L0_ffn_in['sw1'], 'L0_ffn_sb1': _L0_ffn_in['sb1'], 'L0_ffn_sw3': _L0_ffn_in['sw3'], 'L0_ffn_sb3': _L0_ffn_in['sb3'], 'L0_ffn_sw2': _L0_ffn_in['sw2'], 'L0_ffn_sb2': _L0_ffn_in['sb2']}
    _x0 = _d['L0_attn_x']
    _d['L0_attn_x'] = jax.random.normal(jax.random.fold_in(jax.random.key(seed), 1), (4, 2048, 256), dtype=_x0.dtype)
    del _x0
    return _d

def reference(L0_attn_x, L0_attn_w_q, L0_attn_w_k, L0_attn_w_v, L0_attn_w_o, L0_attn_b_o, L0_ffn_gate_w, L0_ffn_gate_b, L0_ffn_w1, L0_ffn_b1, L0_ffn_w3, L0_ffn_b3, L0_ffn_w2, L0_ffn_b2, L0_ffn_sw1, L0_ffn_sb1, L0_ffn_sw3, L0_ffn_sb3, L0_ffn_sw2, L0_ffn_sb2):

    def _L0_attn_ref(x, w_q, w_k, w_v, w_o, b_o):
        import jax, jax.numpy as jnp
        import numpy as np
        IMG_SIZE = 224
        PATCH_SIZE = 16
        CONTEXT_LEN = 79
        LATENT_DIM = 256
        NUM_HEADS = 16
        NUM_PATCHES = (IMG_SIZE // PATCH_SIZE) ** 2
        SEQ_LEN = NUM_PATCHES + CONTEXT_LEN
        BATCH = 8

        def prefix_lm_mask(num_img_patches, total):
            m = np.tril(np.ones((total, total), dtype=np.float32))
            m[:num_img_patches, :num_img_patches] = 1.0
            return jnp.asarray(m)
        B, S, D = x.shape
        H = NUM_HEADS
        hd = D // H
        q = (x @ w_q.T).reshape(B, S, H, hd).transpose(0, 2, 1, 3)
        k = (x @ w_k.T).reshape(B, S, H, hd).transpose(0, 2, 1, 3)
        v = (x @ w_v.T).reshape(B, S, H, hd).transpose(0, 2, 1, 3)
        scores = jnp.einsum('bhqd,bhkd->bhqk', q, k) / jnp.sqrt(jnp.float32(hd))
        mask = prefix_lm_mask(NUM_PATCHES, S)
        scores = jnp.where(mask == 0, jnp.float32(-jnp.inf), scores)
        attn = jax.nn.softmax(scores, axis=-1)
        ctx = jnp.einsum('bhqk,bhkd->bhqd', attn, v)
        ctx = ctx.transpose(0, 2, 1, 3).reshape(B, S, D)
        return ctx @ w_o.T + b_o

    def _L0_ffn_ref(x, gate_w, gate_b, w1, b1, w3, b3, w2, b2, sw1, sb1, sw3, sb3, sw2, sb2):
        import jax, jax.numpy as jnp
        import numpy as np
        E = 8
        TOP_K = 2
        ROUTE_SCALE = 1.0
        ALPHA = 1.702
        LIMIT = 7.0
        D = 256
        F = 256
        B, S = (2, 256)

        def swiglu(h):
            g = jnp.minimum(h[..., ::2], LIMIT)
            l = jnp.clip(h[..., 1::2], -LIMIT, LIMIT)
            return g * jax.nn.sigmoid(ALPHA * g) * (l + 1.0)
        if __name__ == '__main__':
            out = reference(**setup_inputs())
            print(out.shape, out.dtype)
        inp_shape = x.shape
        xt = x.reshape(-1, D)
        logits = xt @ gate_w.T
        scores = jax.nn.softmax(logits.astype(jnp.float32), axis=-1)
        biased = scores + gate_b.astype(jnp.float32)
        idx = jax.lax.top_k(biased, TOP_K)[1]
        weights = (jnp.take_along_axis(scores, idx, axis=-1) * ROUTE_SCALE).astype(x.dtype)
        cw = jnp.sum(jax.nn.one_hot(idx, E, dtype=x.dtype) * weights[..., None], axis=1)
        h1 = jnp.einsum('td,efd->etf', xt, w1) + b1[:, None, :]
        h3 = jnp.einsum('td,efd->etf', xt, w3) + b3[:, None, :]
        a = swiglu(h1 * h3)
        y = jnp.einsum('etf,edf->etd', a, w2) + b2[:, None, :]
        routed = jnp.einsum('te,etd->td', cw, y)
        sh = swiglu((xt @ sw1.T + sb1) * (xt @ sw3.T + sb3))
        shared = sh @ sw2.T + sb2
        return (routed + shared).reshape(inp_shape)
    x = L0_attn_x
    x = x + _layernorm(_L0_attn_ref(_layernorm(x, axis=-1), L0_attn_w_q, L0_attn_w_k, L0_attn_w_v, L0_attn_w_o, L0_attn_b_o), axis=-1)
    x = x + _layernorm(_L0_ffn_ref(_layernorm(x, axis=-1), L0_ffn_gate_w, L0_ffn_gate_b, L0_ffn_w1, L0_ffn_b1, L0_ffn_w3, L0_ffn_b3, L0_ffn_w2, L0_ffn_b2, L0_ffn_sw1, L0_ffn_sb1, L0_ffn_sw3, L0_ffn_sb3, L0_ffn_sw2, L0_ffn_sb2), axis=-1)
    return x

_drawn_inputs = setup_inputs


def setup_inputs(seed=0):
    import zlib

    import numpy as np

    out = dict(_drawn_inputs(seed))
    spreads = {}
    factors = {'L0_ffn_b1': 8.0,
     'L0_ffn_b3': 8.0,
     'L0_ffn_b2': 21.446,
     'L0_ffn_sb1': 8.0,
     'L0_ffn_sb3': 8.0,
     'L0_ffn_sb2': 8.0}
    for name, (base, spread) in spreads.items():
        noise = np.random.default_rng([zlib.crc32(name.encode()), seed]).standard_normal(out[name].shape)
        drawn = base * np.exp(spread * noise) if base else spread * noise
        out[name] = jnp.asarray(drawn.astype(out[name].dtype))
    for name, factor in factors.items():
        out[name] = (out[name] * factor).astype(out[name].dtype)
    return out
```

```python
from contextlib import ExitStack

import numpy as np
import concourse.bass as bass
from concourse import mybir

P = 128
B, SEQ, D = 4, 2048, 256
T = B * SEQ
H, HD = 16, 16
PREFIX = (224 // 16) ** 2
E, F = 8, 256
KT = D // P
CH = 512
TPC = CH // P
NCH = T // CH
BCH = SEQ // CH
NT = T // P
PAIRS = H // 2
EPS = 1e-5
ALPHA, LIMIT = 1.702, 7.0

Q_SLOTS = (0, 0, 0, 1, 1, 2)
K_SLOTS = (0, 1, 2, 0, 1, 0)
SROWS = len(Q_SLOTS) * HD
GUARD = 3
KROWS = SROWS + GUARD
MASKED = -1.0e38

VA_W = 64
VB_ONE = 1 + 2 * HD
VB_W = 2 * VB_ONE + VA_W
VB_M = VA_W + VB_ONE

ROUTED = 2 * T // CH + E
ROWS = (NCH + ROUTED) * CH
NEC = NCH + ROUTED
W13 = KT * 2 * 2 * F
W2 = KT * D
WM = W13 + W2
FB = 2 * F // P
WROW = WM + 2 * FB + D

F32 = mybir.dt.float32
F32R = mybir.dt.float32r
BF16 = mybir.dt.bfloat16
I32 = mybir.dt.int32
U32 = mybir.dt.uint32
ALU = mybir.AluOpType
ACT = mybir.ActivationFunctionType
AX_X = mybir.AxisListType.X

assert NEC % 2 == 0


class Phase:

    def __init__(self, nc, ctx, name):
        self.nc, self.ctx, self.name = nc, ctx, name
        self.sems = []
        ctx.callback(self.end)

    def end(self):
        if self.sems:
            self.nc.clear_and_free_semaphores(self.sems)
            self.nc.all_engine_barrier()

    def sb(self, name, shape, dt=F32):
        return self.ctx.enter_context(self.nc.sbuf_tensor(f"{self.name}_{name}", shape, dt))

    def sb2(self, name, shape, dt=F32):
        return [self.sb(f"{name}{s}", shape, dt) for s in range(2)]

    def ps(self, name, shape):
        return self.ctx.enter_context(self.nc.psum_tensor(f"{self.name}_{name}", shape, F32))

    def sem(self, name):
        self.sems.append(self.nc.alloc_semaphore(f"{self.name}_{name}"))
        return self.sems[-1]

    def sem2(self, name):
        return [self.sem(f"{name}{s}") for s in range(2)]


def in_pairs(eng, count, step):
    step(0, 0, (0, 1), None)
    step(0, 1, (1, 0), (0, 0))
    step(1, 0, (1, 1), (0, 1))
    with eng.Fori(1, count // 2 - 2) as it:
        step(it, 1, (it + 1, 0), (it, 0))
        step(it + 1, 0, (it + 1, 1), (it, 1))
    last = count // 2 - 1
    step(last - 1, 1, (last, 0), (last - 1, 0))
    step(last, 0, (last, 1), (last - 1, 1))
    step(last, 1, None, (last, 0))


def in_rounds(eng, count, round_):
    round_(0)
    with eng.Fori(1, count) as it:
        round_(it)


def chunk_of(n, s):
    return bass.ds(n * 2 + s, 1)


def bcast(ap, at, shape):
    return ap.unsqueeze(at).broadcast_to(shape)


def build(nc, x, w_q, w_k, w_v, w_o, b_o, gate_w, gate_b, w1, b1, w3, b3, w2, b2,
          sw1, sb1, sw3, sb3, sw2, sb2, out):
    def dram(name, shape, dt=F32):
        return nc.dram_tensor(name, shape, dt, kind="Internal").ap()

    qk_parts = dram("qk_parts", (NCH, 2, 3, D, CH), BF16)
    va_scr = dram("va_scr", (NCH, PAIRS, P, TPC * 2 * VA_W), BF16)
    vb_scr = dram("vb_scr", (NCH, PAIRS, P, TPC * VB_W))
    guard = dram("guard", (B, PAIRS, GUARD, 2, SEQ), BF16)
    ctx_scr = dram("ctx_scr", (T, D))
    x1_scr = dram("x1_scr", (NCH, P, TPC, D))
    rows_in = dram("rows_in", (ROWS, D))
    rows_out = dram("rows_out", (ROWS, D))
    w_scr = dram("w_scr", (E + 1, P, WROW))

    x_ch = x.rearrange("b (c j p) d -> (b c) p j d", j=TPC, p=P)
    out_ch = out.rearrange("b (c j p) d -> (b c) p j d", j=TPC, p=P)
    ctx_ch = ctx_scr.rearrange("(c j p) d -> c p j d", j=TPC, p=P)
    rin_ch = rows_in.rearrange("(c j p) d -> c p j d", j=TPC, p=P)
    rout_ch = rows_out.rearrange("(c j p) d -> c p j d", j=TPC, p=P)

    with ExitStack() as whole:
        keep = Phase(nc, whole, "keep")
        ident = keep.sb("ident", [P, P])
        power = keep.sb("power", [P, TPC])
        heads_of = keep.sb("heads_of", [P, 4, 2 * H], BF16)
        norms = keep.sb("norms", [2 * H, NCH])
        wqkv = [keep.sb(f"wqkv_{h}", [P, KT, 3 * D], F32R) for h in ("hi", "lo")]
        wo = [keep.sb(f"wo_{h}", [P, KT, D], F32R) for h in ("hi", "lo")]
        gw = [keep.sb(f"gw_{h}", [P, KT, E], F32R) for h in ("hi", "lo")]
        logits = keep.sb("logits", [P, NT, E])
        weight = keep.sb("weight", [P, 2, NT])
        slot = keep.sb("slot", [P, 2, NT], I32)
        expert_of = keep.sb("expert_of", [1, NEC], I32)

        prepare_weights(nc, ident, power, heads_of, wqkv, wo, gw, w_q, w_k, w_v, w_o, gate_w,
                        w1, b1, w3, b3, w2, b2, sw1, sb1, sw3, sb3, sw2, sb2, w_scr, rows_in, guard)
        project(nc, ident, power, heads_of, norms, wqkv, x_ch, qk_parts, va_scr, vb_scr)
        find_maxima(nc, ident, norms, qk_parts, guard)
        attend(nc, ident, qk_parts, va_scr, vb_scr, guard, ctx_ch)
        attention_out(nc, ident, power, wo, gw, b_o, x_ch, ctx_ch, x1_scr, rin_ch, logits)
        route(nc, gate_b, logits, weight, slot, expert_of)
        experts(nc, ident, rin_ch, rows_in, rout_ch, w_scr, slot, expert_of)
        combine(nc, power, rout_ch, rows_out, x1_scr, weight, slot, out_ch)


def prepare_weights(nc, ident, power, heads_of, wqkv, wo, gw, w_q, w_k, w_v, w_o, gate_w,
                    w1, b1, w3, b3, w2, b2, sw1, sb1, sw3, sb3, sw2, sb2, w_scr, rows_in, guard):
    with ExitStack() as ctx:
        ph = Phase(nc, ctx, "prep")
        raw = ph.sb("raw", [P, 4, KT, D])
        graw = ph.sb("graw", [E, D])
        zeros = ph.sb("zeros", [P, 4096])
        ein = ph.sb2("ein", [P, 2 * FB + KT, D])
        eout = ph.sb2("eout", [P, WROW])
        pt = [ph.ps(f"pt{i}", [P, KT * D]) for i in range(3)]
        pe5 = [ph.ps(f"pe{i}", [P, CH]) for i in range(5)]
        made = ph.sem("constants_made")
        iz = ph.sem("identity_zeroed")
        loaded = ph.sem("weights_loaded")
        turned = ph.sem("weights_transposed")
        hi_done = ph.sem("hi_done")
        lo_done = ph.sem("lo_done")
        zeroed = ph.sem("scratch_zeroed")
        e_loaded = ph.sem2("expert_loaded")
        e_turned = ph.sem("expert_bank_transposed")
        e_copied_a = ph.sem("expert_bank_copied_by_scalar")
        e_copied_v = ph.sem("expert_bank_copied_by_vector")
        e_stored = ph.sem2("expert_stored")
        dst = [(wqkv, 0), (wqkv, 1), (wqkv, 2), (wo, 0)]

        def half(pair, which, m):
            buf, at = pair
            return buf[which][:, :, at * D:(at + 1) * D]

        def sources(e):
            if e is None:
                return sw1, sb1, sw3, sb3, sw2, sb2
            pick = lambda w: w[bass.ds(e, 1)].rearrange(
                "a r c -> (a r) c" if len(w.shape) == 3 else "a r -> (a r)")
            return tuple(pick(w) for w in (w1, b1, w3, b3, w2, b2))

        with nc.Block() as block:
            @block.gpsimd
            def _(pool):
                nc.gpsimd.memset(ident[:], 0.0).then_inc(iz, 1)
                nc.gpsimd.memset(power[:], -0.5).then_inc(made, 1)
                nc.gpsimd.memset(zeros[:], 0.0).then_inc(made, 1)
                nc.gpsimd.memset(heads_of[:], 0.0).then_inc(iz, 1)
                pool.wait_ge(iz, 2)
                nc.gpsimd.affine_select(out=ident[:], in_=ident[:], compare_op=ALU.not_equal, fill=1.0,
                                        base=0, pattern=[[-1, P]], channel_multiplier=1).then_inc(made, 1)
                for m in range(4):
                    at = m * (P // HD)
                    own = heads_of[:, m, at:at + P // HD]
                    nc.gpsimd.memset(own, 1.0).then_inc(iz, 1)
                    pool.wait_ge(iz, 3 + 3 * m)
                    nc.gpsimd.affine_select(out=own, in_=own, compare_op=ALU.is_ge, fill=0.0, base=0,
                                            pattern=[[-HD, P // HD]], channel_multiplier=1).then_inc(iz, 1)
                    pool.wait_ge(iz, 4 + 3 * m)
                    nc.gpsimd.affine_select(out=own, in_=own, compare_op=ALU.is_ge, fill=0.0, base=HD - 1,
                                            pattern=[[HD, P // HD]], channel_multiplier=-1).then_inc(iz, 1)
                pool.wait_ge(iz, 2 + 3 * 4)
                pool.wait_ge(made, 3)
                sorted_rows = rows_in[NCH * CH:, :].rearrange("(n p r) d -> n p (r d)", p=P, r=16)
                for i in range(ROUTED * CH // P // 16):
                    pool.dma_start(sorted_rows[i], zeros[:]).then_inc(zeroed, 16)
                pool.dma_start(guard.rearrange("b q g h (u t) -> (b q g) (h u t)", u=1),
                               zeros[0:B * PAIRS * GUARD, 0:SEQ].bitcast(BF16)).then_inc(zeroed, 16)
                pool.wait_ge(zeroed, 16 * (ROUTED * CH // P // 16 + 1))

            @block.sync
            def _(sp):
                for m, w in enumerate((w_q, w_k, w_v, w_o)):
                    sp.dma_start(raw[:, m], w.rearrange("(o p) i -> p o i", p=P)).then_inc(loaded, 16)
                sp.dma_start(graw[:], gate_w).then_inc(loaded, 16)

                def load(e, n, s):
                    a1, c1, a3, c3, a2, c2 = sources(e)
                    sp.wait_ge(e_stored[s], n * 16)
                    for i, w in enumerate((a1, a3)):
                        for par in range(2):
                            sp.dma_start(ein[s][:, i * FB + 2 * par:i * FB + 2 * par + 2, :],
                                         w.rearrange("(o p two) d -> two p o d", p=P, two=2)[par])\
                                .then_inc(e_loaded[s], 16)
                    sp.dma_start(ein[s][:, 2 * FB:, :], a2.rearrange("(o p) f -> p o f", p=P))\
                        .then_inc(e_loaded[s], 16)
                    for i, c in enumerate((c1, c3)):
                        for par in range(2):
                            with nc.allow_non_contiguous_dma(reason="a few biases, one to a partition"):
                                sp.dma_start(eout[s][:, WM + i * FB + 2 * par:WM + i * FB + 2 * par + 2],
                                             c.rearrange("(o p two) -> two p o", p=P, two=2)[par])\
                                    .then_inc(e_loaded[s], 16)
                    sp.dma_start(eout[s][:, WM + 2 * FB:], bcast(c2, 0, [P, D])).then_inc(e_loaded[s], 16)

                in_rounds(sp, E // 2, lambda it: [load(it * 2 + s, it, s) for s in range(2)])
                load(None, E // 2, 0)
                sp.wait_ge(e_stored[0], 16 * (E // 2 + 1))
                sp.wait_ge(e_stored[1], 16 * (E // 2))

            @block.tensor
            def _(pe):
                pe.wait_ge(made, 3)
                for m in range(4):
                    pe.wait_ge(loaded, 16 * 5)
                    if m >= 3:
                        pe.wait_ge(lo_done, m - 2)
                    for k in range(KT):
                        for o in range(KT):
                            last = nc.tensor.transpose(pt[m % 3][:, k * D + o * P:k * D + (o + 1) * P],
                                                       raw[:, m, o, k * P:(k + 1) * P], ident[:])
                    last.then_inc(turned, 1)
                pe.wait_ge(lo_done, 2)
                for k in range(KT):
                    last = nc.tensor.transpose(pt[1][:, k * E:(k + 1) * E], graw[:, k * P:(k + 1) * P],
                                               ident[0:E, 0:E])
                last.then_inc(turned, 1)

                def turn(n, s, banks):
                    pe.wait_ge(e_loaded[s], (n + 1) * 160)
                    for i in range(5):
                        if i < 2 or i == 4:
                            pe.wait_ge(e_copied_a, banks[0])
                        else:
                            pe.wait_ge(e_copied_v, banks[1])
                        if i < 4:
                            w, k = i // 2, i % 2
                            for o in range(FB):
                                last = nc.tensor.transpose(pe5[i][:, o * P:(o + 1) * P],
                                                           ein[s][:, w * FB + o, k * P:(k + 1) * P], ident[:])
                        else:
                            for k in range(KT):
                                for o in range(KT):
                                    last = nc.tensor.transpose(
                                        pe5[i][:, k * D + o * P:k * D + (o + 1) * P],
                                        ein[s][:, 2 * FB + o, k * P:(k + 1) * P], ident[:])
                        last.then_inc(e_turned, 1)

                in_rounds(pe, E // 2, lambda it: [turn(it, s, ((it * 2 + s) * 3, (it * 2 + s) * 2)) for s in range(2)])
                turn(E // 2, 0, (E * 3, E * 2))

            @block.scalar
            def _(act):
                for m in range(4):
                    act.wait_ge(turned, m + 1)
                    nc.scalar.activation(half(dst[m], 0, m), pt[m % 3][:].rearrange("p (k o) -> p k o", k=KT),
                                         ACT.Copy).then_inc(hi_done, 1)
                act.wait_ge(turned, 5)
                nc.scalar.activation(gw[0][:], pt[1][:, 0:KT * E].rearrange("p (k o) -> p k o", k=KT),
                                     ACT.Copy).then_inc(hi_done, 1)

                def copy(e, n, s, k):
                    act.wait_ge(e_stored[s], n * 16)
                    for i, at in ((0, 0), (1, 2 * F), (4, W13)):
                        act.wait_ge(e_turned, k * 5 + i + 1)
                        nc.scalar.activation(eout[s][:, at:at + CH], pe5[i][:], ACT.Copy)\
                            .then_inc(e_copied_a, 1)
                    act.wait_ge(e_copied_a, k * 3 + 3)
                    act.wait_ge(e_copied_v, k * 2 + 2)
                    act.wait_ge(e_loaded[s], (n + 1) * 160)
                    act.dma_start(w_scr[bass.ds(e, 1)].rearrange("a p w -> (a p) w"), eout[s][:])\
                        .then_inc(e_stored[s], 16)

                in_rounds(act, E // 2, lambda it: [copy(it * 2 + s, it, s, it * 2 + s) for s in range(2)])
                copy(E, E // 2, 0, E)

            @block.vector
            def _(dve):
                for m in range(4):
                    dve.wait_ge(hi_done, m + 1)
                    nc.vector.tensor_tensor(half(dst[m], 1, m), pt[m % 3][:].rearrange("p (k o) -> p k o", k=KT),
                                            half(dst[m], 0, m).bitcast(F32), ALU.subtract).then_inc(lo_done, 1)
                dve.wait_ge(hi_done, 5)
                nc.vector.tensor_tensor(gw[1][:], pt[1][:, 0:KT * E].rearrange("p (k o) -> p k o", k=KT),
                                        gw[0][:].bitcast(F32), ALU.subtract).then_inc(lo_done, 1)

                def copy(n, s, k):
                    dve.wait_ge(e_stored[s], n * 16)
                    for i in (2, 3):
                        dve.wait_ge(e_turned, k * 5 + i + 1)
                        nc.vector.tensor_copy(eout[s][:, i * CH:(i + 1) * CH], pe5[i][:])\
                            .then_inc(e_copied_v, 1)

                in_rounds(dve, E // 2, lambda it: [copy(it, s, it * 2 + s) for s in range(2)])
                copy(E // 2, 0, E)


def stats_of(nc, dve, src, stats, mv, n, s, stats_done, stats_seen, mv_done, mv_before=0, per=1):
    base = (n * per + mv_before) * TPC
    for j in range(TPC):
        nc.vector.bn_stats(stats[:, j], src[:, j]).then_inc(stats_done[s], 1)
    dve.wait_ge(stats_done[s], base + TPC)
    dve.sem_inc(stats_seen, 1)
    for j in range(TPC):
        nc.vector.bn_aggr(mv[:, j], stats[:, j]).then_inc(mv_done[s], 1)


def inverse_roots(nc, pool, power, s, mv, std, rstd, mv_done, mv_seen, std_done, rstd_done, k):
    pool.wait_ge(mv_done[s], (k + 1) * TPC)
    pool.sem_inc(mv_seen, 1)
    nc.gpsimd.tensor_scalar(std[s][:], mv[s][:, :, 1], EPS, None, ALU.add).then_inc(std_done[s], 1)
    pool.wait_ge(std_done[s], k + 1)
    nc.gpsimd.tensor_tensor(rstd[s][:], std[s][:], power[:], ALU.pow).then_inc(rstd_done[s], 1)


def transposes(nc, psum, src, ident):
    for k in range(KT):
        for j in range(TPC):
            last = nc.tensor.transpose(psum[:, k, j * P:(j + 1) * P], src[:, j, k * P:(k + 1) * P], ident[:])
    return last


PARTS3 = ((0, 0), (0, 1), (1, 0))


def product(nc, psum, left, right, lsl, rsl):
    steps = [(k, a, b) for k in range(KT) for a, b in PARTS3]
    for i, (k, a, b) in enumerate(steps):
        last = nc.tensor.matmul(psum, left[a][:, k, lsl], right[b][:, k, rsl],
                                start=(i == 0), stop=(i == len(steps) - 1))
    return last


def project(nc, ident, power, heads_of, norms, wqkv, x_ch, qk_parts, va_scr, vb_scr):
    with ExitStack() as ctx:
        ph = Phase(nc, ctx, "proj")
        xin = ph.sb2("xin", [P, TPC, D])
        xn = ph.sb2("xn", [P, TPC, D])
        stats = ph.sb2("stats", [P, TPC, 6])
        mv = ph.sb2("mv", [P, TPC, 2])
        std = ph.sb2("std", [P, TPC])
        rstd = ph.sb2("rstd", [P, TPC])
        xt = [[ph.sb(f"xt{s}_{h}", [P, KT, CH], F32R) for h in ("hi", "lo")] for s in range(2)]
        qk = ph.sb2("qk", [P, 3, 4, CH], BF16)
        square = ph.sb("square", [P, 4, CH], BF16)
        rest = ph.sb2("rest", [P, 2, CH])
        va = ph.sb2("va", [P, PAIRS, TPC, 2, VA_W], BF16)
        vb = ph.sb2("vb", [P, PAIRS, TPC, VB_W], F32R)
        vrest = ph.sb("vrest", [P, 2, PAIRS, TPC, HD])
        psT = ph.ps("psT", [P, KT, CH])
        psP = [ph.ps(f"psP{i}", [P, 2 * CH]) for i in range(3)]
        cleared = ph.sem("values_cleared")
        x_loaded, x_normed = ph.sem2("x_loaded"), ph.sem2("x_normed")
        stats_done, mv_done = ph.sem2("stats_done"), ph.sem2("mv_done")
        stats_seen, mv_seen = ph.sem("stats_seen"), ph.sem("mv_seen")
        std_done, rstd_done = ph.sem2("std_done"), ph.sem2("rstd_done")
        turned, xt_done, lo_done = ph.sem2("x_turned"), ph.sem2("xt_hi_done"), ph.sem2("xt_lo_done")
        q_done, v_done = ph.sem2("qk_product_done"), ph.sem2("v_product_done")
        q1, qr1, q2, q3 = (ph.sem2(f"q_{n}") for n in ("part1", "rest1", "part2", "part3"))
        v1, vh, vr1, v2, v3, vl = (ph.sem2(f"v_{n}") for n in ("part1", "hi", "rest1", "part2", "part3", "lo"))
        squared, summed, bounded = ph.sem2("squared"), ph.sem2("norms_summed"), ph.sem2("norms_bounded")
        qk_stored, v_stored = ph.sem2("qk_stored"), ph.sem2("v_stored")

        def v_psum(h):
            return psP[2][:].rearrange("p (j q h d) -> p h q j d", j=TPC, q=PAIRS, h=2)[:, h]

        def va_part(s, h, part):
            return va[s][:, :, :, h, 1 + part * HD:1 + (part + 1) * HD]

        def vb_part(s, h, part):
            at = h * (VB_ONE + VA_W) + 1 + part * HD
            return vb[s][:, :, :, at:at + HD]

        def after(n):
            return not (isinstance(n, int) and n == NCH // 2 - 1)

        with nc.Block() as block:
            @block.sync
            def _(sp):
                def load(n, s):
                    sp.wait_ge(x_normed[s], n * TPC)
                    sp.dma_start(xin[s][:], x_ch[chunk_of(n, s)].rearrange("a p j d -> p (a j) d"))\
                        .then_inc(x_loaded[s], 16)

                def step(n, s, nxt, prv):
                    if prv is None:
                        load(0, 0)
                        load(0, 1)
                    if after(n):
                        load(n + 1, s)
                    sp.wait_ge(q3[s], n * 2 + 2)
                    for side in range(2):
                        for part in range(3):
                            sp.dma_start(
                                qk_parts[chunk_of(n, s), side, part].rearrange("a (h r) t -> r (a h) t", r=P),
                                qk[s][:, part, 2 * side:2 * side + 2, :]).then_inc(qk_stored[s], 16)
                    sp.wait_ge(v3[s], n * 2 + 2)
                    sp.wait_ge(vl[s], n * 2 + 2)
                    sp.dma_start(va_scr[chunk_of(n, s)].rearrange("a q p w -> p (a q) w"),
                                 va[s][:].rearrange("p q j h w -> p q (j h w)")).then_inc(v_stored[s], 16)
                    sp.dma_start(vb_scr[chunk_of(n, s)].rearrange("a q p w -> p (a q) w"),
                                 vb[s][:].bitcast(F32).rearrange("p q j w -> p q (j w)"))\
                        .then_inc(v_stored[s], 16)

                in_pairs(sp, NCH, step)
                for s in range(2):
                    sp.wait_ge(qk_stored[s], NCH // 2 * 96)
                    sp.wait_ge(v_stored[s], NCH // 2 * 32)

            @block.gpsimd
            def _(pool):
                for s in range(2):
                    nc.gpsimd.memset(va[s][:].bitcast(F32), 0.0).then_inc(cleared, 1)
                    nc.gpsimd.memset(vb[s][:].bitcast(F32), 0.0).then_inc(cleared, 1)
                pool.wait_ge(cleared, 4)
                for s in range(2):
                    nc.gpsimd.memset(va[s][:, :, :, :, 0:1], 1.0).then_inc(cleared, 1)
                    for h in range(2):
                        at = h * (VB_ONE + VA_W)
                        nc.gpsimd.memset(vb[s][:, :, :, at:at + 1].bitcast(F32), 1.0).then_inc(cleared, 1)

                in_pairs(pool, NCH, lambda n, s, nxt, prv: inverse_roots(
                    nc, pool, power, s, mv, std, rstd, mv_done, mv_seen, std_done, rstd_done, n))

            @block.tensor
            def _(pe):
                def turn(n, s):
                    pe.wait_ge(x_normed[s], n * TPC + TPC)
                    if s == 1:
                        pe.wait_ge(lo_done[0], n + 1)
                        pe.wait_ge(bounded[1], n)
                    else:
                        pe.wait_ge(lo_done[1], n)
                        pe.wait_ge(bounded[0], n)
                    transposes(nc, psT, xn[s], ident).then_inc(turned[s], 1)

                def step(n, s, nxt, prv):
                    if prv is None:
                        turn(0, 0)
                    pe.wait_ge(lo_done[s], n + 1)
                    for side in range(2):
                        if s == 1:
                            pe.wait_ge(qr1[0], n * 2 + side + 1)
                        else:
                            pe.wait_ge(qr1[1], n * 2)
                        for m in range(2):
                            at = (2 * side + m) * P
                            last = product(nc, psP[side][:, m * CH:(m + 1) * CH], wqkv, xt[s],
                                           slice(at, at + P), slice(0, CH))
                        last.then_inc(q_done[s], 1)
                    if nxt is not None:
                        turn(*nxt)
                    if s == 1:
                        pe.wait_ge(vl[0], n * 2 + 2)
                    else:
                        pe.wait_ge(vl[1], n * 2)
                    for j in range(TPC):
                        last = product(nc, psP[2][:, j * D:(j + 1) * D], xt[s], wqkv, slice(j * P, (j + 1) * P),
                                       slice(2 * D, 3 * D))
                    last.then_inc(v_done[s], 1)
                    if nxt is not None:
                        pe.wait_ge(lo_done[nxt[1]], nxt[0] + 1)
                    else:
                        pe.wait_ge(bounded[prv[1]], prv[0] + 1)
                    pe.wait_ge(squared[s], n * 2 + 2)
                    for m in range(4):
                        last = nc.tensor.matmul(psT[0:2 * H, 0, :], heads_of[:, m], square[:, m],
                                                start=(m == 0), stop=(m == 3))
                    last.then_inc(summed[s], 1)

                in_pairs(pe, NCH, step)

            @block.scalar
            def _(act):
                def hi(n, s):
                    act.wait_ge(turned[s], n + 1)
                    nc.scalar.activation(xt[s][0][:], psT[:], ACT.Copy).then_inc(xt_done[s], 1)

                def step(n, s, nxt, prv):
                    if prv is None:
                        hi(0, 0)
                    act.wait_ge(qk_stored[s], n * 96)
                    for side in range(2):
                        act.wait_ge(q_done[s], n * 2 + side + 1)
                        prod = psP[side][:].rearrange("p (m t) -> p m t", m=2)
                        if side == 0 and prv is not None:
                            act.wait_ge(summed[prv[1]], prv[0] + 1)
                        nc.scalar.activation(square[:, 2 * side:2 * side + 2], prod, ACT.Square)\
                            .then_inc(squared[s], 1)
                        nc.scalar.activation(qk[s][:, 0, 2 * side:2 * side + 2], prod, ACT.Copy).then_inc(q1[s], 1)
                    if nxt is not None:
                        hi(*nxt)
                    for side in range(2):
                        act.wait_ge(qr1[s], n * 2 + side + 1)
                        nc.scalar.activation(qk[s][:, 1, 2 * side:2 * side + 2], rest[side][:], ACT.Copy)\
                            .then_inc(q2[s], 1)
                    act.wait_ge(v_stored[s], n * 32)
                    act.wait_ge(cleared, 10)
                    act.wait_ge(v_done[s], n + 1)
                    for h in range(2):
                        nc.scalar.activation(va_part(s, h, 0), v_psum(h), ACT.Copy).then_inc(v1[s], 1)
                    for h in range(2):
                        nc.scalar.activation(vb_part(s, h, 0), v_psum(h), ACT.Copy).then_inc(vh[s], 1)
                    for h in range(2):
                        act.wait_ge(vr1[s], n * 2 + h + 1)
                        nc.scalar.activation(va_part(s, h, 1), vrest[:, h], ACT.Copy).then_inc(v2[s], 1)

                in_pairs(act, NCH, step)

            @block.vector
            def _(dve):
                V = nc.vector

                def measure(n, s):
                    dve.wait_ge(x_loaded[s], n * 16 + 16)
                    stats_of(nc, dve, xin[s], stats[s], mv[s], n, s, stats_done, stats_seen, mv_done)

                def normalize(n, s):
                    dve.wait_ge(rstd_done[s], n + 1)
                    dve.wait_ge(turned[s], n)
                    for j in range(TPC):
                        V.tensor_scalar(xn[s][:, j], xin[s][:, j], mv[s][:, j, 0:1], rstd[s][:, j:j + 1],
                                        ALU.subtract, ALU.mult).then_inc(x_normed[s], 1)

                def lo(n, s):
                    dve.wait_ge(xt_done[s], n + 1)
                    V.tensor_tensor(xt[s][1][:], psT[:], xt[s][0][:].bitcast(F32), ALU.subtract)\
                        .then_inc(lo_done[s], 1)

                def bound(n, s):
                    dve.wait_ge(summed[s], n + 1)
                    V.tensor_reduce(norms[:, bass.ds(n * 2 + s, 1)], psT[0:2 * H, 0, :], AX_X, ALU.max)\
                        .then_inc(bounded[s], 1)

                def step(n, s, nxt, prv):
                    if prv is None:
                        measure(0, 0)
                        normalize(0, 0)
                        lo(0, 0)
                        measure(0, 1)
                    if prv is not None:
                        bound(*prv)
                    if nxt is not None:
                        normalize(*nxt)
                    for side in range(2):
                        dve.wait_ge(q1[s], n * 2 + side + 1)
                        V.tensor_tensor(rest[side][:], psP[side][:].rearrange("p (m t) -> p m t", m=2),
                                        qk[s][:, 0, 2 * side:2 * side + 2], ALU.subtract).then_inc(qr1[s], 1)
                    if nxt is not None:
                        lo(*nxt)
                    for side in range(2):
                        dve.wait_ge(q2[s], n * 2 + side + 1)
                        V.tensor_tensor(qk[s][:, 2, 2 * side:2 * side + 2], rest[side][:],
                                        qk[s][:, 1, 2 * side:2 * side + 2], ALU.subtract).then_inc(q3[s], 1)
                    dve.wait_ge(v1[s], n * 2 + 2)
                    dve.wait_ge(vh[s], n * 2 + 2)
                    for h in range(2):
                        V.tensor_tensor(vrest[:, h], v_psum(h), va_part(s, h, 0), ALU.subtract).then_inc(vr1[s], 1)
                    for h in range(2):
                        V.tensor_tensor(vb_part(s, h, 1), v_psum(h), vb_part(s, h, 0).bitcast(F32), ALU.subtract)\
                            .then_inc(vl[s], 1)
                    if after(n):
                        measure(n + 1, s)
                    for h in range(2):
                        dve.wait_ge(v2[s], n * 2 + h + 1)
                        V.tensor_tensor(va_part(s, h, 2), vrest[:, h], va_part(s, h, 1), ALU.subtract)\
                            .then_inc(v3[s], 1)
                    if nxt is None:
                        bound(n, s)

                in_pairs(dve, NCH, step)


SAFE = 40.0


def find_maxima(nc, ident, norms, qk_parts, guard):
    with ExitStack() as ctx:
        ph = Phase(nc, ctx, "max")
        greatest = ph.sb("greatest", [2 * H, 1])
        row = ph.sb("row", [1, 2 * H])
        bounds = ph.sb("bounds", [1, H])
        bound = ph.sb("bound", [1, 1])
        flagf = ph.sb("flagf", [1, 1])
        flag = ph.sb("flag", [1, 1], I32)
        qs = ph.sb("qs", [SROWS, SEQ], BF16)
        ks = ph.sb("ks", [SROWS, SEQ], BF16)
        identb = ph.sb("identb", [P, P], BF16)
        tri = ph.sb("tri", [P, P], BF16)
        pre = ph.sb("pre", [P, P], BF16)
        top = ph.sb("top", [P, SEQ // P])
        minus = ph.sb("minus", [P, SEQ // P])
        rest = ph.sb("rest", [SEQ // P, 2, P])
        part = ph.sb("part", [SEQ // P, GUARD, P], BF16)
        pss = ph.ps("scores", [P, SEQ])
        pst = ph.ps("turned", [P, P])
        zeroed, made = ph.sem("masks_zeroed"), ph.sem("masks_made")
        step, row_turned = ph.sem("bound_steps"), ph.sem("row_turned")
        loaded, scored, tops, negated = (ph.sem(n) for n in ("head_loaded", "scores_ready", "maxima", "negated"))
        minus_turned, cut, stored = (ph.sem(n) for n in ("maxima_turned", "parts_cut", "parts_stored"))
        HEADS = 2 * B * PAIRS
        QT = SEQ // P
        LOADS = 2 * len(Q_SLOTS)

        def all_heads(eng, head):
            needed = eng.value_load(flag[0:1, 0:1], min_val=0, max_val=1)
            with eng.If(needed > 0):
                with eng.Fori(0, B) as b:
                    with eng.Fori(0, PAIRS) as pair:
                        for h in range(2):
                            head(b, pair, h, b * H + pair * 2 + h)
                if eng is nc.scalar:
                    eng.wait_ge(stored, HEADS * 16 * GUARD + 1)

        with nc.Block() as block:
            @block.vector
            def _(dve):
                V = nc.vector
                V.tensor_reduce(greatest[:], norms[:], AX_X, ALU.max).then_inc(step, 1)
                dve.wait_ge(row_turned, 1)
                V.tensor_copy(row[:], pst[0:1, 0:2 * H]).then_inc(step, 1)
                dve.wait_ge(step, 2)
                V.tensor_tensor(bounds[:], row[:, 0:H], row[:, H:], ALU.mult).then_inc(step, 1)
                dve.wait_ge(step, 3)
                V.tensor_reduce(bound[:], bounds[:], AX_X, ALU.max).then_inc(step, 1)
                dve.wait_ge(step, 4)
                V.tensor_scalar(flagf[:], bound[:], SAFE * SAFE * HD, None, ALU.is_gt).then_inc(step, 1)
                dve.wait_ge(step, 5)
                V.tensor_copy(flag[:], flagf[:]).then_inc(step, 1)

            @block.tensor
            def _(pe):
                pe.wait_ge(step, 1)
                nc.tensor.transpose(pst[0:1, 0:2 * H], greatest[:], ident[0:2 * H, 0:2 * H]).then_inc(row_turned, 1)

            @block.gpsimd
            def _(pool):
                nc.gpsimd.memset(identb[:], 0.0).then_inc(zeroed, 1)
                nc.gpsimd.memset(tri[:], 0.0).then_inc(zeroed, 1)
                nc.gpsimd.memset(pre[:], 0.0).then_inc(zeroed, 1)
                pool.wait_ge(zeroed, 3)
                nc.gpsimd.affine_select(out=identb[:], in_=identb[:], compare_op=ALU.not_equal, fill=1.0,
                                        base=0, pattern=[[-1, P]], channel_multiplier=1).then_inc(made, 1)
                left = PREFIX - P
                nc.gpsimd.affine_select(out=tri[:], in_=tri[:], compare_op=ALU.is_ge, fill=MASKED,
                                        base=0, pattern=[[-1, P]], channel_multiplier=1).then_inc(made, 1)
                nc.gpsimd.affine_select(out=pre[:, left:], in_=pre[:, left:], compare_op=ALU.is_ge, fill=MASKED,
                                        base=-left, pattern=[[-1, P - left]], channel_multiplier=1)\
                    .then_inc(made, 1)

        with nc.Block() as block:
            @block.sync
            def _(sp):
                sp.sem_inc(stored, 1)

                def head(b, pair, h, n):
                    sp.wait_ge(scored, n * QT + 1)
                    for side, buf, slots in ((0, qs, Q_SLOTS), (1, ks, K_SLOTS)):
                        for i, p in enumerate(slots):
                            sp.dma_start(
                                buf[i * HD:(i + 1) * HD].rearrange("r (c t) -> r c t", c=BCH),
                                qk_parts[bass.ds(b * BCH, BCH), side, p, bass.ds(pair * 2 * HD + h * HD, HD), :]
                                .rearrange("c r t -> r c t")).then_inc(loaded, 16)

                all_heads(sp, head)

            @block.tensor
            def _(pe):
                pe.sem_inc(scored, 1)

                def head(b, pair, h, n):
                    pe.wait_ge(loaded, (n + 1) * 16 * LOADS)
                    for t in range(QT):
                        keys = max((t + 1) * P, PREFIX)
                        masked = (t + 1) * P > PREFIX
                        pe.wait_ge(tops, n * QT + t + 1)
                        for c in range(0, keys, CH):
                            end = min(c + CH, keys)
                            diagonal = masked and end == keys
                            last = nc.tensor.matmul(pss[:, c:end], qs[:, t * P:(t + 1) * P], ks[:, c:end],
                                                    start=True, stop=not diagonal)
                            if diagonal:
                                mask = pre if t * P < PREFIX else tri
                                last = nc.tensor.matmul(pss[:, keys - P:keys], identb[:], mask[:],
                                                        start=False, stop=True)
                        last.then_inc(scored, 1)
                    pe.wait_ge(negated, n + 1)
                    nc.tensor.transpose(pst[0:QT, :], minus[:], ident[:]).then_inc(minus_turned, 1)

                all_heads(pe, head)

            @block.vector
            def _(dve):
                V = nc.vector
                dve.sem_inc(tops, 1)

                def head(b, pair, h, n):
                    for t in range(QT):
                        keys = max((t + 1) * P, PREFIX)
                        dve.wait_ge(scored, n * QT + t + 2)
                        V.tensor_reduce(top[:, t:t + 1], pss[:, 0:keys], AX_X, ALU.max).then_inc(tops, 1)
                    dve.wait_ge(tops, n * QT + QT + 1)
                    V.tensor_scalar(minus[:], top[:], -1.0, None, ALU.mult).then_inc(negated, 1)
                    dve.wait_ge(minus_turned, n + 1)
                    dve.wait_ge(stored, n * 16 * GUARD + 1)
                    V.tensor_copy(part[:, 0], pst[0:QT, :]).then_inc(cut, 1)
                    dve.wait_ge(cut, n * 5 + 1)
                    V.tensor_tensor(rest[:, 0], pst[0:QT, :], part[:, 0], ALU.subtract).then_inc(cut, 1)
                    dve.wait_ge(cut, n * 5 + 2)
                    V.tensor_copy(part[:, 1], rest[:, 0]).then_inc(cut, 1)
                    dve.wait_ge(cut, n * 5 + 3)
                    V.tensor_tensor(rest[:, 1], rest[:, 0], part[:, 1], ALU.subtract).then_inc(cut, 1)
                    dve.wait_ge(cut, n * 5 + 4)
                    V.tensor_copy(part[:, 2], rest[:, 1]).then_inc(cut, 1)

                all_heads(dve, head)

            @block.scalar
            def _(act):
                def head(b, pair, h, n):
                    act.wait_ge(cut, n * 5 + 5)
                    for g in range(GUARD):
                        act.dma_start(guard[bass.ds(b, 1), bass.ds(pair, 1), g, h].rearrange(
                            "a q (t p) -> t (a q p)", p=P), part[:, g]).then_inc(stored, 16)

                all_heads(act, head)


def units():
    for c in range(BCH):
        for kt in range(TPC * (c + 1)):
            first = max(0, kt * P - c * CH)
            if kt * P < PREFIX:
                first = 0
            yield c, kt, first


UNITS = list(units())
LAST_UNIT = {c: max(i for i, u in enumerate(UNITS) if u[0] == c) for c in range(BCH)}
SBUFS = 3


def attend(nc, ident, qk_parts, va_scr, vb_scr, guard, ctx_ch):
    with ExitStack() as ctx:
        ph = Phase(nc, ctx, "att")
        qs = ph.sb2("qs", [KROWS, 2, SEQ], BF16)
        ks = ph.sb2("ks", [KROWS, 2, SEQ], BF16)
        va = ph.sb2("va", [P, SEQ // P, 2 * VA_W], BF16)
        vb = ph.sb2("vb", [P, SEQ // P, VB_W], F32R)
        prob = [ph.sb(f"prob{i}", [P, 2, CH]) for i in range(SBUFS)]
        low = [ph.sb(f"low{i}", [P, 2, CH], F32R) for i in range(SBUFS)]
        osb = ph.sb2("osb", [P, CH])
        csum = ph.sb2("csum", [P, 2 * TPC, HD])
        rden = ph.sb2("rden", [P, 2 * TPC])
        cout = ph.sb2("cout", [P, TPC, 2 * HD])
        identb = ph.sb("identb", [P, P], BF16)
        tri = ph.sb("tri", [P, P], BF16)
        pre = ph.sb("pre", [P, 2, P], BF16)
        pss = [ph.ps(f"scores{i}", [P, 2, CH]) for i in range(SBUFS)]
        pso = [ph.ps(f"out{i}", [P, CH]) for i in range(2)]
        made, zeroed = ph.sem("masks_made"), ph.sem("masks_zeroed")
        loaded = ph.sem2("heads_loaded")
        scored, exped, lowed, used = (ph.sem(n) for n in ("scores_ready", "probs_ready", "low_ready", "probs_used"))
        o_ready, o_copied, o_turned = ph.sem("out_ready"), ph.sem("out_copied"), ph.sem("out_turned")
        summed, inverted, c_done = ph.sem("parts_summed"), ph.sem("denominators_inverted"), ph.sem("context_done")
        stored = ph.sem2("context_stored")
        free = ph.sem("context_buffer_free")
        heads_used = ph.sem2("heads_used")
        nu = len(UNITS)
        LOADS = 4 * len(Q_SLOTS) + 3
        stream = [(s, i) for s in range(2) for i in range(nu)]
        chunks = [(s, c) for s in range(2) for c in range(BCH)]
        nb = len(stream)
        end_of = {s * nu + LAST_UNIT[c]: s * BCH + c for s, c in chunks}

        def turned(k, it):
            s, c = chunks[k]
            return (heads_used[s], it + 2) if c == BCH - 1 else (o_turned, it * (2 * BCH - 2) + k - s + 2)


        with nc.Block() as block:
            @block.gpsimd
            def _(pool):
                nc.gpsimd.memset(identb[:], 0.0).then_inc(zeroed, 1)
                nc.gpsimd.memset(tri[:], 0.0).then_inc(zeroed, 1)
                nc.gpsimd.memset(pre[:], 0.0).then_inc(zeroed, 1)
                pool.wait_ge(zeroed, 3)
                nc.gpsimd.affine_select(out=identb[:], in_=identb[:], compare_op=ALU.not_equal, fill=1.0,
                                        base=0, pattern=[[-1, P]], channel_multiplier=1).then_inc(made, 1)
                nc.gpsimd.affine_select(out=tri[:], in_=tri[:], compare_op=ALU.is_ge, fill=MASKED,
                                        base=0, pattern=[[1, P]], channel_multiplier=-1).then_inc(made, 1)
                left = PREFIX - P
                nc.gpsimd.affine_select(out=pre[:, 0], in_=pre[:, 0], compare_op=ALU.is_gt, fill=MASKED,
                                        base=left, pattern=[[0, P]], channel_multiplier=-1).then_inc(made, 1)
                nc.gpsimd.affine_select(out=pre[:, 1, left:], in_=pre[:, 1, left:], compare_op=ALU.is_ge,
                                        fill=MASKED, base=left, pattern=[[1, P - left]],
                                        channel_multiplier=-1).then_inc(made, 1)
                nc.gpsimd.affine_select(out=pre[:, 1, 0:left], in_=pre[:, 1, 0:left], compare_op=ALU.is_gt,
                                        fill=MASKED, base=left, pattern=[[0, left]],
                                        channel_multiplier=-1).then_inc(made, 1)
                pool.sem_inc(free, 2)
                with pool.Fori(0, B) as b:
                    with pool.Fori(0, PAIRS // 2) as q:
                        n = b * (PAIRS // 2) + q
                        for k, (s, c) in enumerate(chunks):
                            pool.wait_ge(c_done, n * len(chunks) + k + 1)
                            pool.dma_start(
                                ctx_ch[bass.ds(b * BCH + c, 1), :, :, bass.ds((q * 2 + s) * 2 * HD, 2 * HD)]
                                .rearrange("a p j d -> p (a j) d"), cout[k % 2][:]).then_inc(stored[k % 2], 16)
                            pool.wait_ge(stored[k % 2], (n * BCH + k // 2 + 1) * 16)
                            pool.sem_inc(free, 1)

            @block.sync
            def _(sp):
                def load(b, n, pair, s):
                    sp.wait_ge(heads_used[s], n + 1)
                    heads = bass.ds(pair * 2 * HD, 2 * HD)
                    for side, buf, slots in ((0, qs, Q_SLOTS), (1, ks, K_SLOTS)):
                        for i, part in enumerate(slots):
                            for h in range(2):
                                sp.dma_start(
                                    buf[s][i * HD:(i + 1) * HD, h].rearrange("r (c t) -> r c t", c=BCH),
                                    qk_parts[bass.ds(b * BCH, BCH), side, part, bass.ds(pair * 2 * HD + h * HD, HD), :]
                                    .rearrange("c r t -> r c t")).then_inc(loaded[s], 16)
                    sp.dma_start(qs[s][SROWS:KROWS], guard[bass.ds(b, 1), bass.ds(pair, 1)].rearrange(
                        "a q g h t -> (a q g) h t")).then_inc(loaded[s], 16)
                    sp.dma_start(va[s][:].rearrange("p (c j) w -> p c (j w)", c=BCH),
                                 va_scr[bass.ds(b * BCH, BCH), bass.ds(pair, 1)].rearrange(
                                     "c q p w -> p (c q) w")).then_inc(loaded[s], 16)
                    sp.dma_start(vb[s][:].bitcast(F32).rearrange("p (c j) w -> p c (j w)", c=BCH),
                                 vb_scr[bass.ds(b * BCH, BCH), bass.ds(pair, 1)].rearrange(
                                     "c q p w -> p (c q) w")).then_inc(loaded[s], 16)

                with sp.Fori(0, B) as b:
                    with sp.Fori(0, PAIRS // 2) as q:
                        for s in range(2):
                            load(b, b * (PAIRS // 2) + q, q * 2 + s, s)

            @block.tensor
            def _(pe):
                pe.wait_ge(made, 7)
                for primed in (used, o_turned, *heads_used):
                    pe.sem_inc(primed, 1)

                def scores(g, it):
                    s, i = stream[g]
                    c, kt, first = UNITS[i]
                    if i == 0:
                        pe.wait_ge(loaded[s], (it + 1) * 16 * LOADS)
                    pe.wait_ge(exped, it * nb + max(0, g - SBUFS + 1) + 1)
                    diag = c * TPC <= kt
                    mask = None
                    if kt * P < PREFIX:
                        if c == 0 and (kt + 1) * P > PREFIX:
                            mask, at, w = pre[:].rearrange("p a b -> p (a b)"), 0, 2 * P
                    elif diag:
                        mask, at, w = tri[:], first, P
                    for h in range(2):
                        last = nc.tensor.matmul(pss[g % SBUFS][:, h, first:], ks[s][:, h, kt * P:(kt + 1) * P],
                                                qs[s][:, h, c * CH + first:(c + 1) * CH],
                                                start=True, stop=mask is None)
                        if mask is not None:
                            last = nc.tensor.matmul(pss[g % SBUFS][:, h, at:at + w], identb[:], mask,
                                                    start=False, stop=True)
                    last.then_inc(scored, 1)

                def values(g, it):
                    s, i = stream[g]
                    c, kt, first = UNITS[i]
                    k = s * BCH + c
                    o = pso[k % 2]
                    pe.wait_ge(lowed, it * nb + g + 1)
                    if kt == 0:
                        pe.wait_ge(summed, it * len(chunks) + max(0, k - 1) + 1)
                        pe.wait_ge(inverted, it * len(chunks) + max(0, k - 1) + 1)
                    upper = prob[g % SBUFS][:].bitcast(BF16)
                    for h in range(2):
                        nc.tensor.matmul(o[h * VA_W:(h + 1) * VA_W, first:], va[s][:, kt, h * VA_W:(h + 1) * VA_W],
                                         upper[:, h, 2 * first + 1:2 * CH:2], start=(kt == 0), stop=False,
                                         skip_group_check=True)
                    for h in range(2):
                        at = h * VB_ONE
                        last = nc.tensor.matmul(o[0:VB_M, first:], vb[s][:, kt, at:at + VB_M],
                                                low[g % SBUFS][:, h, first:], start=False,
                                                stop=(i == LAST_UNIT[c]), skip_group_check=True)
                    last.then_inc(used, 1)

                def turn(k, it):
                    pe.wait_ge(o_copied, it * len(chunks) + k + 1)
                    for j in range(TPC):
                        last = nc.tensor.transpose(pso[k % 2][:, j * P:(j + 1) * P],
                                                   osb[k % 2][:, j * P:(j + 1) * P], ident[:])
                    last.then_inc(turned(k, it)[0], 1)

                with pe.Fori(0, B * PAIRS // 2) as it:
                    scores(0, it)
                    scores(1, it)
                    for g in range(nb):
                        if g + 2 < nb:
                            scores(g + 2, it)
                        values(g, it)
                        if g - 2 in end_of:
                            turn(end_of[g - 2], it)
                    for g in (nb - 2, nb - 1):
                        if g in end_of:
                            turn(end_of[g], it)

            @block.scalar
            def _(act):
                act.sem_inc(exped, 1)
                with act.Fori(0, B * PAIRS // 2) as it:
                    for g in range(nb + 3):
                        if g < nb:
                            first = UNITS[stream[g][1]][2]
                            act.wait_ge(scored, it * nb + g + 1)
                            act.wait_ge(used, it * nb + max(0, g - SBUFS + 1) + 1)
                            nc.scalar.activation(prob[g % SBUFS][:, :, first:], pss[g % SBUFS][:, :, first:],
                                                 ACT.Exp, scale=HD ** -0.5).then_inc(exped, 1)
                        if g - 2 in end_of:
                            k = end_of[g - 2]
                            act.wait_ge(used, it * nb + g)
                            if k >= 2:
                                act.wait_ge(*turned(k - 2, it))
                            elif k == 1:
                                act.wait_ge(heads_used[1], it + 1)
                            else:
                                act.wait_ge(o_turned, it * (2 * BCH - 2) + 1)
                            nc.scalar.activation(osb[k % 2][:], pso[k % 2][:], ACT.Copy).then_inc(o_copied, 1)

            @block.vector
            def _(dve):
                def finish(k, it):
                    dve.wait_ge(*turned(k, it))
                    o = pso[k % 2][:].rearrange("p (g w) -> p g w", w=VA_W)
                    nc.vector.tensor_reduce(csum[k % 2][:], o[:, :, 1:1 + 3 * HD].rearrange(
                        "p g (a d) -> p g d a", a=3), AX_X, ALU.add).then_inc(summed, 1)
                    nc.vector.reciprocal(rden[k % 2][:], o[:, :, 0]).then_inc(inverted, 1)
                    dve.wait_ge(summed, it * len(chunks) + k + 2)
                    dve.wait_ge(inverted, it * len(chunks) + k + 2)
                    dve.wait_ge(free, it * len(chunks) + k + 1)
                    nc.vector.tensor_tensor(cout[k % 2][:].rearrange("p j (h d) -> p (j h) d", h=2), csum[k % 2][:],
                                            rden[k % 2][:].unsqueeze(2).broadcast_to([P, 2 * TPC, HD]),
                                            ALU.mult).then_inc(c_done, 1)

                for s in range(2):
                    nc.vector.memset(ks[s][SROWS:KROWS], 1.0).then_inc(made, 1)

                dve.sem_inc(summed, 1)
                dve.sem_inc(inverted, 1)
                with dve.Fori(0, B * PAIRS // 2) as it:
                    for g in range(nb + 5):
                        if g < nb:
                            first = UNITS[stream[g][1]][2]
                            dve.wait_ge(exped, it * nb + g + 2)
                            dve.wait_ge(used, it * nb + max(0, g - SBUFS + 1) + 1)
                            nc.vector.tensor_tensor(
                                low[g % SBUFS][:, :, first:], prob[g % SBUFS][:, :, first:],
                                prob[g % SBUFS][:].bitcast(BF16)[:, :, 2 * first + 1:2 * CH:2],
                                ALU.subtract).then_inc(lowed, 1)
                        if g - 4 in end_of:
                            finish(end_of[g - 4], it)


def attention_out(nc, ident, power, wo, gw, b_o, x_ch, ctx_ch, x1_scr, rin_ch, logits):
    with ExitStack() as ctx:
        ph = Phase(nc, ctx, "out")
        cin = ph.sb2("cin", [P, TPC, D])
        xin = ph.sb2("xin", [P, TPC, D])
        at = ph.sb2("att", [P, TPC, D])
        an = ph.sb2("attn", [P, TPC, D])
        x1 = ph.sb2("x1", [P, TPC, D])
        xn = ph.sb2("xn", [P, TPC, D])
        bias = ph.sb("bias", [P, D])
        stats = ph.sb2("stats", [P, TPC, 6])
        mv = ph.sb2("mv", [P, TPC, 2])
        std = ph.sb2("std", [P, TPC])
        rstd = ph.sb2("rstd", [P, TPC])
        ct = [[ph.sb(f"ct{s}_{h}", [P, KT, CH], F32R) for h in ("hi", "lo")] for s in range(2)]
        nt = [[ph.sb(f"nt{s}_{h}", [P, KT, CH], F32R) for h in ("hi", "lo")] for s in range(2)]
        psT = ph.ps("psT", [P, KT, CH])
        psN = ph.ps("psN", [P, KT, CH])
        psO = [ph.ps(f"psO{i}", [P, 2, D]) for i in range(2)]
        psG = [ph.ps(f"psG{i}", [P, TPC, E]) for i in range(2)]
        b_loaded = ph.sem("bias_loaded")
        c_loaded, x_loaded = ph.sem2("context_loaded"), ph.sem2("x_loaded")
        c_turned, c_hi, c_lo = ph.sem2("context_turned"), ph.sem2("context_hi"), ph.sem2("context_lo")
        n_turned, n_hi, n_lo = ph.sem2("normed_turned"), ph.sem2("normed_hi"), ph.sem2("normed_lo")
        o_done, biased = ph.sem2("projected"), ph.sem2("bias_added")
        stats_done, mv_done = ph.sem2("stats_done"), ph.sem2("mv_done")
        stats_seen, mv_seen = ph.sem("stats_seen"), ph.sem("mv_seen")
        std_done, rstd_done = ph.sem2("std_done"), ph.sem2("rstd_done")
        a_normed, x1_done, x_normed = ph.sem2("att_normed"), ph.sem2("x1_done"), ph.sem2("x1_normed")
        g_done, g_kept = ph.sem2("logits_done"), ph.sem2("logits_kept")
        x1_stored, xn_stored = ph.sem2("x1_stored"), ph.sem2("normed_stored")

        with nc.Block() as block:
            @block.sync
            def _(sp):
                sp.dma_start(bias[:], bcast(b_o, 0, [P, D])).then_inc(b_loaded, 16)

                def load(n, s):
                    sp.wait_ge(c_turned[s], n)
                    sp.dma_start(cin[s][:], ctx_ch[chunk_of(n, s)].rearrange("a p j d -> p (a j) d"))\
                        .then_inc(c_loaded[s], 16)
                    sp.wait_ge(x1_done[s], n)
                    sp.dma_start(xin[s][:], x_ch[chunk_of(n, s)].rearrange("a p j d -> p (a j) d"))\
                        .then_inc(x_loaded[s], 16)

                def step(n, s, nxt, prv):
                    if prv is None:
                        load(0, 0)
                    if nxt is not None:
                        load(*nxt)
                    sp.wait_ge(x1_done[s], n + 1)
                    sp.dma_start(x1_scr[chunk_of(n, s)].rearrange("a p j d -> p (a j) d"), x1[s][:])\
                        .then_inc(x1_stored[s], 16)
                    sp.wait_ge(x_normed[s], (n + 1) * TPC)
                    sp.dma_start(rin_ch[chunk_of(n, s)].rearrange("a p j d -> p (a j) d"), xn[s][:])\
                        .then_inc(xn_stored[s], 16)

                in_pairs(sp, NCH, step)
                for s in range(2):
                    sp.wait_ge(x1_stored[s], NCH // 2 * 16)
                    sp.wait_ge(xn_stored[s], NCH // 2 * 16)

            @block.gpsimd
            def _(pool):
                def step(n, s, nxt, prv):
                    for half in range(2):
                        inverse_roots(nc, pool, power, s, mv, std, rstd, mv_done, mv_seen, std_done, rstd_done, n * 2 + half)

                in_pairs(pool, NCH, step)

            @block.tensor
            def _(pe):
                def turn(n, s):
                    pe.wait_ge(c_loaded[s], n * 16 + 16)
                    if s == 1:
                        pe.wait_ge(c_lo[0], n + 1)
                    else:
                        pe.wait_ge(c_lo[1], n)
                    transposes(nc, psT, cin[s], ident).then_inc(c_turned[s], 1)

                def router(n, s):
                    pe.wait_ge(x_normed[s], n * TPC + TPC)
                    if s == 1:
                        pe.wait_ge(n_lo[0], n + 1)
                    else:
                        pe.wait_ge(n_lo[1], n)
                    transposes(nc, psN, xn[s], ident).then_inc(n_turned[s], 1)
                    pe.wait_ge(n_lo[s], n + 1)
                    pe.wait_ge(g_kept[s], n)
                    for j in range(TPC):
                        last = product(nc, psG[s][:, j], nt[s], gw, slice(j * P, (j + 1) * P), slice(0, E))
                    last.then_inc(g_done[s], 1)

                def step(n, s, nxt, prv):
                    if prv is None:
                        turn(0, 0)
                    pe.wait_ge(c_lo[s], n + 1)
                    for t in range(2):
                        if s == 1:
                            pe.wait_ge(biased[0], n * 2 + t + 1)
                        else:
                            pe.wait_ge(biased[1], n * 2)
                        for u in range(2):
                            j = 2 * t + u
                            last = product(nc, psO[t][:, u], ct[s], wo, slice(j * P, (j + 1) * P), slice(0, D))
                        last.then_inc(o_done[s], 1)
                    if nxt is not None:
                        turn(*nxt)
                    if prv is not None:
                        router(*prv)
                    if nxt is None:
                        router(n, s)

                in_pairs(pe, NCH, step)

            @block.scalar
            def _(act):
                def context_hi(n, s):
                    act.wait_ge(c_turned[s], n + 1)
                    nc.scalar.activation(ct[s][0][:], psT[:], ACT.Copy).then_inc(c_hi[s], 1)

                def normed_hi(n, s):
                    act.wait_ge(n_turned[s], n + 1)
                    nc.scalar.activation(nt[s][0][:], psN[:], ACT.Copy).then_inc(n_hi[s], 1)

                def step(n, s, nxt, prv):
                    if prv is None:
                        context_hi(0, 0)
                    if nxt is not None:
                        context_hi(*nxt)
                    if prv is not None:
                        normed_hi(*prv)
                    if nxt is None:
                        normed_hi(n, s)

                in_pairs(act, NCH, step)

            @block.vector
            def _(dve):
                dve.wait_ge(b_loaded, 16)

                def context_lo(n, s):
                    dve.wait_ge(c_hi[s], n + 1)
                    nc.vector.tensor_tensor(ct[s][1][:], psT[:], ct[s][0][:].bitcast(F32), ALU.subtract)\
                        .then_inc(c_lo[s], 1)

                def logits_out(n, s):
                    dve.wait_ge(n_hi[s], n + 1)
                    nc.vector.tensor_tensor(nt[s][1][:], psN[:], nt[s][0][:].bitcast(F32), ALU.subtract)\
                        .then_inc(n_lo[s], 1)
                    dve.wait_ge(g_done[s], n + 1)
                    nc.vector.tensor_copy(logits[:, bass.ds(n * (2 * TPC) + s * TPC, TPC), :], psG[s][:])\
                        .then_inc(g_kept[s], 1)

                def norm(n, s, src, dst, half, done, before=None):
                    stats_of(nc, dve, src, stats[s], mv[s], n, s, stats_done, stats_seen, mv_done, half, 2)
                    dve.wait_ge(rstd_done[s], n * 2 + half + 1)
                    for j in range(TPC):
                        nc.vector.tensor_scalar(dst[:, j], src[:, j], mv[s][:, j, 0:1], rstd[s][:, j:j + 1],
                                                ALU.subtract, ALU.mult).then_inc(done[s], 1)

                def step(n, s, nxt, prv):
                    if prv is None:
                        context_lo(0, 0)
                    for t in range(2):
                        dve.wait_ge(o_done[s], n * 2 + t + 1)
                        nc.vector.tensor_tensor(at[s][:, 2 * t:2 * t + 2], psO[t][:],
                                                bcast(bias[:], 1, [P, 2, D]), ALU.add).then_inc(biased[s], 1)
                    if nxt is not None:
                        context_lo(*nxt)
                    if prv is not None:
                        logits_out(*prv)
                    dve.wait_ge(biased[s], n * 2 + 2)
                    norm(n, s, at[s], an[s], 0, a_normed)
                    dve.wait_ge(a_normed[s], (n + 1) * TPC)
                    dve.wait_ge(x_loaded[s], n * 16 + 16)
                    dve.wait_ge(x1_stored[s], n * 16)
                    nc.vector.tensor_tensor(x1[s][:], an[s][:], xin[s][:], ALU.add).then_inc(x1_done[s], 1)
                    dve.wait_ge(x1_done[s], n + 1)
                    dve.wait_ge(xn_stored[s], n * 16)
                    norm(n, s, x1[s], xn[s], 1, x_normed)
                    if nxt is None:
                        logits_out(n, s)

                in_pairs(dve, NCH, step)


def route(nc, gate_b, logits, weight, slot, expert_of):
    with ExitStack() as ctx:
        ph = Phase(nc, ctx, "route")
        gb = ph.sb("gate_b", [P, E])
        top = ph.sb("top", [P, NT])
        ex = ph.sb("ex", [P, NT, E])
        den = ph.sb("den", [P, NT])
        score = ph.sb("score", [P, NT, E])
        biased = ph.sb("biased", [P, NT, E])
        best = ph.sb("best", [P, NT, 8])
        which = ph.sb("which", [P, NT, 8], U32)
        whichf = ph.sb("whichf", [P, NT, 8])
        lane = ph.sb("lane", [P, E])
        hot = ph.sb("hot", [P, 2, NT, E])
        both = ph.sb("both", [P, NT, E])
        tmp = ph.sb("tmp", [P, 2, NT, E])
        before = ph.sb("before", [P, P])
        ones = ph.sb("ones", [P, NT])
        onesq = ph.sb("onesq", [P, P])
        total = ph.sb("total", [P, NT, E])
        upto = ph.sb("upto", [P, E, NT])
        at = ph.sb("at", [P, NT, E])
        cnt = ph.sb("cnt", [P, E])
        cnti = ph.sb("cnti", [P, E], I32)
        shr = ph.sb("shr", [P, E], I32)
        padded = ph.sb("padded", [P, E])
        ends = ph.sb("ends", [P, E])
        base = ph.sb("base", [P, E])
        slotf = ph.sb("slotf", [P, 2, NT])
        chunk0 = ph.sb("chunk0", [1, ROUTED])
        past = ph.sb("past", [1, ROUTED, E])
        eidf = ph.sb("eidf", [1, NEC])
        psp = ph.ps("psp", [P, NT, E])
        pst = ph.ps("pst", [P, NT, E])
        made, zeroed, loaded = ph.sem("made"), ph.sem("zeroed"), ph.sem("loaded")
        step, exped, counted = ph.sem("vector_steps"), ph.sem("exp_done"), ph.sem("counted")
        shift = CH.bit_length() - 1

        with nc.Block() as block:
            @block.sync
            def _(sp):
                sp.dma_start(gb[:], bcast(gate_b, 0, [P, E])).then_inc(loaded, 16)

            @block.gpsimd
            def _(pool):
                nc.gpsimd.memset(ones[:], 1.0).then_inc(made, 1)
                nc.gpsimd.memset(onesq[:], 1.0).then_inc(zeroed, 1)
                nc.gpsimd.iota(lane[:], pattern=[[1, E]], base=0, channel_multiplier=0,
                               allow_small_or_imprecise_dtypes=True).then_inc(made, 1)
                nc.gpsimd.iota(chunk0[:], pattern=[[CH, ROUTED]], base=0, channel_multiplier=0,
                               allow_small_or_imprecise_dtypes=True).then_inc(made, 1)
                pool.wait_ge(zeroed, 1)
                nc.gpsimd.affine_select(out=before[:], in_=onesq[:], compare_op=ALU.is_gt, fill=0.0,
                                        base=0, pattern=[[1, P]], channel_multiplier=-1).then_inc(made, 1)

            @block.scalar
            def _(act):
                act.wait_ge(step, 2)
                nc.scalar.activation(ex[:], ex[:], ACT.Exp).then_inc(exped, 1)

            @block.tensor
            def _(pe):
                pe.wait_ge(made, 4)
                pe.wait_ge(step, BOTH_STEP)
                nc.tensor.matmul(psp[:].rearrange("p t e -> p (t e)"), before[:],
                                 both[:].rearrange("p t e -> p (t e)"), start=True, stop=True).then_inc(counted, 1)
                nc.tensor.matmul(pst[:].rearrange("p t e -> p (t e)"), onesq[:],
                                 both[:].rearrange("p t e -> p (t e)"), start=True, stop=True).then_inc(counted, 1)

            @block.vector
            def _(dve):
                V = nc.vector
                did = [0]

                def then(ins):
                    ins.then_inc(step, 1)
                    did[0] += 1
                    dve.wait_ge(step, did[0])

                wide = [P, NT, E]
                then(V.tensor_reduce(top[:], logits[:], AX_X, ALU.max))
                then(V.tensor_tensor(ex[:], logits[:], top[:].unsqueeze(2).broadcast_to(wide), ALU.subtract))
                dve.wait_ge(exped, 1)
                then(V.tensor_reduce(den[:], ex[:], AX_X, ALU.add))
                then(V.reciprocal(top[:], den[:]))
                then(V.tensor_tensor(score[:], ex[:], top[:].unsqueeze(2).broadcast_to(wide), ALU.mult))
                dve.wait_ge(loaded, 16)
                then(V.tensor_tensor(biased[:], score[:], bcast(gb[:], 1, wide), ALU.add))
                for t in range(NT):
                    last = V.max(best[:, t], biased[:, t])
                then(last)
                for t in range(NT):
                    last = V.max_index(which[:, t], best[:, t], biased[:, t])
                then(last)
                then(V.tensor_copy(whichf[:], which[:]))
                dve.wait_ge(made, 4)
                for r in range(2):
                    then(V.tensor_tensor(hot[:, r], whichf[:, :, r:r + 1].broadcast_to(wide), bcast(lane[:], 1, wide),
                                         ALU.is_equal))
                then(V.tensor_tensor(both[:], hot[:, 0], hot[:, 1], ALU.add))
                assert did[0] == BOTH_STEP
                for r in range(2):
                    then(V.tensor_tensor(tmp[:, r], hot[:, r], score[:], ALU.mult))
                then(V.tensor_reduce(weight[:], tmp[:], AX_X, ALU.add))
                dve.wait_ge(counted, 2)
                then(V.tensor_copy(total[:], pst[:]))
                for e in range(E):
                    then(V.tensor_tensor_scan(upto[:, e], ones[:], total[:, :, e], 0.0, ALU.mult, ALU.add))
                then(V.tensor_tensor(at[:], upto[:].rearrange("p e t -> p t e"), total[:], ALU.subtract))
                then(V.tensor_tensor(at[:], at[:], psp[:], ALU.add))
                then(V.tensor_scalar(cnt[:], upto[:, :, NT - 1], float(CH - 1), None, ALU.add))
                then(V.tensor_copy(cnti[:], cnt[:]))
                then(V.tensor_scalar(shr[:], cnti[:], shift, shift, ALU.logical_shift_right,
                                     ALU.logical_shift_left))
                then(V.tensor_copy(padded[:], shr[:]))
                then(V.tensor_tensor_scan(ends[:], ones[:, 0:E], padded[:], 0.0, ALU.mult, ALU.add))
                then(V.tensor_tensor(base[:], ends[:], padded[:], ALU.subtract))
                then(V.tensor_scalar(base[:], base[:], float(NCH * CH), None, ALU.add))
                then(V.tensor_tensor(at[:], at[:], bcast(base[:], 1, wide), ALU.add))
                for r in range(2):
                    then(V.tensor_tensor(tmp[:, r], hot[:, r], at[:], ALU.mult))
                then(V.tensor_reduce(slotf[:], tmp[:], AX_X, ALU.add))
                then(V.tensor_copy(slot[:], slotf[:]))
                then(V.tensor_tensor(past[:], chunk0[:].unsqueeze(2).broadcast_to([1, ROUTED, E]),
                                     bcast(ends[0:1, :], 1, [1, ROUTED, E]), ALU.is_ge))
                then(V.memset(eidf[:], float(E)))
                then(V.tensor_reduce(eidf[:, NCH:], past[:], AX_X, ALU.add))
                then(V.tensor_scalar(eidf[:, NCH:], eidf[:, NCH:], float(E - 1), None, ALU.min))
                then(V.tensor_copy(expert_of[:], eidf[:]))


BOTH_STEP = 12


def experts(nc, ident, rin_ch, rows_in, rout_ch, w_scr, slot, expert_of):
    with ExitStack() as ctx:
        ph = Phase(nc, ctx, "moe")
        wraw = ph.sb2("wraw", [P, WROW])
        w = [[ph.sb(f"w{s}_{h}", [P, WM], F32R) for h in ("hi", "lo")] for s in range(2)]
        xin = ph.sb2("xin", [P, TPC, D])
        xt = [[ph.sb(f"xt{s}_{h}", [P, KT, CH], F32R) for h in ("hi", "lo")] for s in range(2)]
        h3 = ph.sb2("h3", [P, CH])
        u = ph.sb("u", [P, FB, CH])
        sig = ph.sb("sig", [P, KT, CH])
        a = ph.sb("a", [P, KT, CH])
        ah = [[ph.sb(f"a{s}_{h}", [P, KT, CH], F32R) for h in ("hi", "lo")] for s in range(2)]
        y = ph.sb2("y", [P, TPC, D])
        wb = ph.sb2("wb", [P, 2 * FB + D])
        sin = ph.sb2("sin", [P, TPC, D])
        sidx = ph.sb2("sidx", [P, 2, TPC], I32)
        psT = ph.ps("psT", [P, KT, CH])
        ps1 = [ph.ps(f"ps1_{i}", [P, CH]) for i in range(2)]
        ps3 = [ph.ps(f"ps3_{i}", [P, CH]) for i in range(2)]
        psY = [ph.ps(f"psY{i}", [P, 2, D]) for i in range(2)]
        w_loaded, x_loaded = ph.sem2("weights_loaded"), ph.sem2("rows_loaded")
        w_hi, w_lo, w_bias = (ph.sem2(n) for n in ("weights_hi", "weights_lo", "biases_copied"))
        turned, x_hi, x_lo = ph.sem2("rows_turned"), ph.sem2("rows_hi"), ph.sem2("rows_lo")
        p1, p3 = ph.sem2("h1_product"), ph.sem2("h3_product")
        h3_done, u_done = ph.sem2("h3_done"), ph.sem2("u_done")
        g_cut, l_cut, sig_done, gs_done, a_done = (ph.sem2(n) for n in
                                                  ("gate_cut", "linear_cut", "sigmoid_done", "gate_done", "a_done"))
        a_hi, a_lo = ph.sem2("a_hi"), ph.sem2("a_lo")
        y_done, y_biased, y_stored = ph.sem2("y_product"), ph.sem2("y_biased"), ph.sem2("y_stored")
        s_loaded, s_index, scattered = ph.sem2("tokens_loaded"), ph.sem2("index_copied"), ph.sem2("tokens_scattered")

        def wk(half, which, k):
            return half[:, (which * KT + k) * 2 * F:(which * KT + k + 1) * 2 * F]

        s_ready = ph.sem("scatter_may_start")

        with nc.Block() as block:
            @block.gpsimd
            def _(pool):
                def round_(it):
                    for s in range(2):
                        pool.wait_ge(scattered[s], it * 2 * TPC * 16)
                        pool.dma_start(sin[s][:], rin_ch[chunk_of(it, s)].rearrange("a p j d -> p (a j) d"))\
                            .then_inc(s_loaded[s], 16)
                        nc.gpsimd.tensor_copy(sidx[s][:], slot[:, :, bass.ds(it * (2 * TPC) + s * TPC, TPC)])\
                            .then_inc(s_index[s], 1)
                        pool.wait_ge(s_loaded[s], it * 16 + 16)
                        pool.wait_ge(s_index[s], it + 1)
                        pool.sem_inc(s_ready, 1)
                        for r in range(2):
                            for j in range(TPC):
                                pool.indirect_dma_start(
                                    out=rows_in, out_offset=bass.IndirectOffsetOnAxis(sidx[s][:, r, j:j + 1], 0),
                                    in_=sin[s][:, j, :], in_offset=None).then_inc(scattered[s], 16)

                in_rounds(pool, NCH // 2, round_)
                for s in range(2):
                    pool.wait_ge(scattered[s], NCH // 2 * 2 * TPC * 16)

            @block.sync
            def _(sp):
                def load(n, s):
                    sp.wait_ge(turned[s], n)
                    sp.dma_start(xin[s][:], rin_ch[chunk_of(n, s)].rearrange("a p j d -> p (a j) d"))\
                        .then_inc(x_loaded[s], 16)
                    sp.wait_ge(w_lo[s], n)
                    sp.wait_ge(w_bias[s], n)
                    e = sp.value_load(expert_of[0:1, chunk_of(n, s)], min_val=0, max_val=E)
                    sp.dma_start(wraw[s][:], w_scr[bass.ds(e, 1)].rearrange("a p w -> (a p) w"))\
                        .then_inc(w_loaded[s], 16)

                in_rounds(sp, NCH // 2, lambda it: [load(it, s) for s in range(2)])
                for s in range(2):
                    sp.wait_ge(scattered[s], NCH // 2 * 2 * TPC * 16)
                with sp.Fori(NCH // 2, NEC // 2) as it:
                    for s in range(2):
                        load(it, s)

            @block.tensor
            def _(pe):
                def turn(n, s):
                    pe.wait_ge(x_loaded[s], n * 16 + 16)
                    if s == 1:
                        pe.wait_ge(x_lo[0], n + 1)
                    else:
                        pe.wait_ge(x_lo[1], n)
                    transposes(nc, psT, xin[s], ident).then_inc(turned[s], 1)

                def hidden(n, s, blocks):
                    pe.wait_ge(x_lo[s], n + 1)
                    pe.wait_ge(w_lo[s], n + 1)
                    for f in blocks:
                        for which, psum, done in ((1, ps3, p3), (0, ps1, p1)):
                            reader = h3_done if which else u_done
                            if f >= 2:
                                pe.wait_ge(reader[s], n * FB + f - 1)
                            elif s == 1:
                                pe.wait_ge(reader[0], n * FB + f + 3)
                            else:
                                pe.wait_ge(reader[1], n * FB)
                            i = 0
                            for k in range(KT):
                                for aa, bb in PARTS3:
                                    last = nc.tensor.matmul(psum[f % 2][:], wk(w[s][aa], which, k)[:, f * P:(f + 1) * P],
                                                            xt[s][bb][:, k], start=(i == 0), stop=(i == 5))
                                    i += 1
                            last.then_inc(done[s], 1)

                def down(n, s):
                    pe.wait_ge(a_lo[s], n + 1)
                    w2s = [w[s][i][:, W13:WM].rearrange("p (k d) -> p k d", k=KT) for i in range(2)]
                    for t in range(2):
                        if s == 1:
                            pe.wait_ge(y_biased[0], n * 2 + t + 1)
                        else:
                            pe.wait_ge(y_biased[1], n * 2)
                        for v in range(2):
                            j = 2 * t + v
                            last = product(nc, psY[t][:, v], ah[s], w2s, slice(j * P, (j + 1) * P), slice(0, D))
                        last.then_inc(y_done[s], 1)

                def step(n, s, nxt, prv):
                    if prv is None:
                        turn(0, 0)
                    if nxt is not None:
                        turn(*nxt)
                    hidden(n, s, range(0, KT))
                    if prv is not None:
                        down(*prv)
                    hidden(n, s, range(KT, FB))
                    if nxt is None:
                        down(n, s)

                in_pairs(pe, NEC, step)

            @block.scalar
            def _(act):
                def prepare(n, s):
                    act.wait_ge(w_loaded[s], n * 16 + 16)
                    act.wait_ge(y_done[s], n * 2)
                    nc.scalar.activation(w[s][0][:], wraw[s][:, 0:WM], ACT.Copy).then_inc(w_hi[s], 1)
                    act.wait_ge(turned[s], n + 1)
                    nc.scalar.activation(xt[s][0][:], psT[:], ACT.Copy).then_inc(x_hi[s], 1)
                    act.wait_ge(y_biased[s], n * 2)
                    nc.scalar.activation(wb[s][:], wraw[s][:, WM:], ACT.Copy).then_inc(w_bias[s], 1)

                def step(n, s, nxt, prv):
                    if prv is None:
                        prepare(0, 0)
                    act.wait_ge(w_bias[s], n + 1)
                    for f in range(FB):
                        act.wait_ge(p3[s], n * FB + f + 1)
                        if f >= 2:
                            act.wait_ge(u_done[s], n * FB + f - 1)
                        elif s == 1:
                            act.wait_ge(u_done[0], n * FB + f + 3)
                        else:
                            act.wait_ge(u_done[1], n * FB)
                        nc.scalar.activation(h3[f % 2][:], ps3[f % 2][:], ACT.Identity,
                                             bias=wb[s][:, FB + f:FB + f + 1]).then_inc(h3_done[s], 1)
                        if f == KT and nxt is not None:
                            prepare(*nxt)
                    act.wait_ge(g_cut[s], n + 1)
                    nc.scalar.activation(sig[:], u[:, 0:KT], ACT.Sigmoid, scale=ALPHA).then_inc(sig_done[s], 1)
                    act.wait_ge(a_done[s], n + 1)
                    act.wait_ge(y_done[s], n * 2)
                    nc.scalar.activation(ah[s][0][:], a[:], ACT.Copy).then_inc(a_hi[s], 1)
                    if prv is not None:
                        store(*prv)
                    if nxt is None:
                        store(n, s)

                def store(n, s):
                    act.wait_ge(y_biased[s], n * 2 + 2)
                    act.dma_start(rout_ch[chunk_of(n, s)].rearrange("a p j d -> p (a j) d"), y[s][:])\
                        .then_inc(y_stored[s], 16)

                in_pairs(act, NEC, step)
                for s in range(2):
                    act.wait_ge(y_stored[s], NEC // 2 * 16)

            @block.vector
            def _(dve):
                V = nc.vector

                def prepare(n, s):
                    dve.wait_ge(w_hi[s], n + 1)
                    V.tensor_tensor(w[s][1][:], wraw[s][:, 0:WM], w[s][0][:].bitcast(F32), ALU.subtract)\
                        .then_inc(w_lo[s], 1)
                    dve.wait_ge(x_hi[s], n + 1)
                    V.tensor_tensor(xt[s][1][:], psT[:], xt[s][0][:].bitcast(F32), ALU.subtract).then_inc(x_lo[s], 1)

                def result(n, s):
                    for t in range(2):
                        dve.wait_ge(y_done[s], n * 2 + t + 1)
                        dve.wait_ge(y_stored[s], n * 16)
                        V.tensor_tensor(y[s][:, 2 * t:2 * t + 2], psY[t][:],
                                        bcast(wb[s][:, 2 * FB:], 1, [P, 2, D]), ALU.add)\
                            .then_inc(y_biased[s], 1)

                def step(n, s, nxt, prv):
                    if prv is None:
                        prepare(0, 0)
                    dve.wait_ge(w_bias[s], n + 1)
                    for f in range(FB):
                        dve.wait_ge(h3_done[s], n * FB + f + 1)
                        dve.wait_ge(p1[s], n * FB + f + 1)
                        if f == 0 and prv is not None:
                            dve.wait_ge(a_done[prv[1]], prv[0] + 1)
                        V.scalar_tensor_tensor(u[:, f], ps1[f % 2][:], wb[s][:, f:f + 1], h3[f % 2][:],
                                               ALU.add, ALU.mult).then_inc(u_done[s], 1)
                        if f == KT - 1:
                            dve.wait_ge(u_done[s], n * FB + KT)
                            V.tensor_scalar(u[:, 0:KT], u[:, 0:KT], LIMIT, None, ALU.min).then_inc(g_cut[s], 1)
                            if prv is not None:
                                result(*prv)
                        if f == KT and nxt is not None:
                            prepare(*nxt)
                    dve.wait_ge(u_done[s], n * FB + FB)
                    V.tensor_scalar(u[:, KT:], u[:, KT:], LIMIT, -LIMIT, ALU.min, ALU.max).then_inc(l_cut[s], 1)
                    dve.wait_ge(sig_done[s], n + 1)
                    V.tensor_tensor(sig[:], sig[:], u[:, 0:KT], ALU.mult).then_inc(gs_done[s], 1)
                    dve.wait_ge(gs_done[s], n + 1)
                    dve.wait_ge(l_cut[s], n + 1)
                    V.scalar_tensor_tensor(a[:], u[:, KT:], 1.0, sig[:], ALU.add, ALU.mult).then_inc(a_done[s], 1)
                    dve.wait_ge(a_hi[s], n + 1)
                    V.tensor_tensor(ah[s][1][:], a[:], ah[s][0][:].bitcast(F32), ALU.subtract).then_inc(a_lo[s], 1)
                    if nxt is None:
                        result(n, s)

                in_pairs(dve, NEC, step)


def combine(nc, power, rout_ch, rows_out, x1_scr, weight, slot, out_ch):
    with ExitStack() as ctx:
        ph = Phase(nc, ctx, "comb")
        sh = ph.sb2("shared", [P, TPC, D])
        x1 = ph.sb2("x1", [P, TPC, D])
        yy = ph.sb2("yy", [P, 2, TPC, D])
        acc = ph.sb2("acc", [P, TPC, D])
        res = ph.sb2("res", [P, TPC, D])
        sidx = ph.sb2("sidx", [P, 2, TPC], I32)
        wgt = ph.sb2("wgt", [P, 2, TPC])
        stats = ph.sb2("stats", [P, TPC, 6])
        mv = ph.sb2("mv", [P, TPC, 2])
        std = ph.sb2("std", [P, TPC])
        rstd = ph.sb2("rstd", [P, TPC])
        loaded, gathered, copied = ph.sem2("loaded"), ph.sem2("gathered"), ph.sem2("index_copied")
        w_copied = ph.sem2("weights_copied")
        first, second = ph.sem2("first_added"), ph.sem2("second_added")
        stats_done, mv_done = ph.sem2("stats_done"), ph.sem2("mv_done")
        stats_seen, mv_seen = ph.sem("stats_seen"), ph.sem("mv_seen")
        std_done, rstd_done, normed = ph.sem2("std_done"), ph.sem2("rstd_done"), ph.sem2("normed")
        done, stored = ph.sem2("done"), ph.sem2("stored")
        ready = ph.sem("gather_may_start")

        with nc.Block() as block:
            @block.gpsimd
            def _(pool):
                def gather(n, s):
                    pool.wait_ge(second[s], n * TPC)
                    nc.gpsimd.tensor_copy(sidx[s][:], slot[:, :, bass.ds(n * (2 * TPC) + s * TPC, TPC)])\
                        .then_inc(copied[s], 1)
                    pool.wait_ge(copied[s], n + 1)
                    pool.sem_inc(ready, 1)
                    for r in range(2):
                        for j in range(TPC):
                            pool.indirect_dma_start(
                                out=yy[s][:, r, j, :], out_offset=None, in_=rows_out,
                                in_offset=bass.IndirectOffsetOnAxis(sidx[s][:, r, j:j + 1], 0))\
                                .then_inc(gathered[s], 16)

                def step(n, s, nxt, prv):
                    if prv is None:
                        gather(0, 0)
                    if nxt is not None:
                        gather(*nxt)
                    inverse_roots(nc, pool, power, s, mv, std, rstd, mv_done, mv_seen, std_done, rstd_done, n)

                in_pairs(pool, NCH, step)

            @block.sync
            def _(sp):
                def load(n, s):
                    sp.wait_ge(done[s], n)
                    sp.dma_start(sh[s][:], rout_ch[chunk_of(n, s)].rearrange("a p j d -> p (a j) d"))\
                        .then_inc(loaded[s], 16)
                    sp.dma_start(x1[s][:], x1_scr[chunk_of(n, s)].rearrange("a p j d -> p (a j) d"))\
                        .then_inc(loaded[s], 16)

                def step(n, s, nxt, prv):
                    if prv is None:
                        load(0, 0)
                    if nxt is not None:
                        load(*nxt)
                    sp.wait_ge(done[s], n + 1)
                    sp.dma_start(out_ch[chunk_of(n, s)].rearrange("a p j d -> p (a j) d"), res[s][:])\
                        .then_inc(stored[s], 16)

                in_pairs(sp, NCH, step)
                for s in range(2):
                    sp.wait_ge(stored[s], NCH // 2 * 16)

            @block.vector
            def _(dve):
                V = nc.vector

                def step(n, s, nxt, prv):
                    V.tensor_copy(wgt[s][:], weight[:, :, bass.ds(n * (2 * TPC) + s * TPC, TPC)])\
                        .then_inc(w_copied[s], 1)
                    dve.wait_ge(w_copied[s], n + 1)
                    dve.wait_ge(loaded[s], n * 32 + 32)
                    dve.wait_ge(gathered[s], (n + 1) * 2 * TPC * 16)
                    for j in range(TPC):
                        V.scalar_tensor_tensor(acc[s][:, j], yy[s][:, 0, j], wgt[s][:, 0, j:j + 1], sh[s][:, j],
                                               ALU.mult, ALU.add).then_inc(first[s], 1)
                    for j in range(TPC):
                        dve.wait_ge(first[s], n * TPC + j + 1)
                        V.scalar_tensor_tensor(acc[s][:, j], yy[s][:, 1, j], wgt[s][:, 1, j:j + 1], acc[s][:, j],
                                               ALU.mult, ALU.add).then_inc(second[s], 1)
                    dve.wait_ge(second[s], n * TPC + TPC)
                    stats_of(nc, dve, acc[s], stats[s], mv[s], n, s, stats_done, stats_seen, mv_done)
                    dve.wait_ge(rstd_done[s], n + 1)
                    for j in range(TPC):
                        V.tensor_scalar(acc[s][:, j], acc[s][:, j], mv[s][:, j, 0:1], rstd[s][:, j:j + 1],
                                        ALU.subtract, ALU.mult).then_inc(normed[s], 1)
                    dve.wait_ge(normed[s], (n + 1) * TPC)
                    dve.wait_ge(stored[s], n * 16)
                    V.tensor_tensor(res[s][:], acc[s][:], x1[s][:], ALU.add).then_inc(done[s], 1)

                in_pairs(dve, NCH, step)


_INS = ("L0_attn_x", "L0_attn_w_q", "L0_attn_w_k", "L0_attn_w_v", "L0_attn_w_o", "L0_attn_b_o",
        "L0_ffn_gate_w", "L0_ffn_gate_b", "L0_ffn_w1", "L0_ffn_b1", "L0_ffn_w3", "L0_ffn_b3",
        "L0_ffn_w2", "L0_ffn_b2", "L0_ffn_sw1", "L0_ffn_sb1", "L0_ffn_sw3", "L0_ffn_sb3",
        "L0_ffn_sw2", "L0_ffn_sb2")


def kernel(**inputs):
    import concourse.bacc as bacc
    from concourse.bass_utils import run_bass_kernel_spmd

    nc = bacc.Bacc("TRN2", target_bir_lowering=False, num_devices=1)
    arrays, args = {}, []
    for name in _INS:
        a = np.ascontiguousarray(inputs[name])
        arrays[name] = a
        args.append(nc.dram_tensor(name, a.shape, mybir.dt.from_np(a.dtype), kind="ExternalInput").ap())
    args.append(nc.dram_tensor("out", (B, SEQ, D), F32, kind="ExternalOutput").ap())
    build(nc, *args)
    r = run_bass_kernel_spmd(nc, [arrays], core_ids=[0])
    return r.results[0]["out"]
```

```python
from contextlib import ExitStack

import numpy as np
import concourse.bass as bass
from concourse import mybir

P = 128
B, SEQ, D = 4, 2048, 256
T = B * SEQ
H, HD = 16, 16
PREFIX = (224 // 16) ** 2
E, F = 8, 256
KT = D // P
CH = 512
TPC = CH // P
NCH = T // CH
BCH = SEQ // CH
NT = T // P
PAIRS = H // 2
EPS = 1e-5
ALPHA, LIMIT = 1.702, 7.0

Q_SLOTS = (0, 0, 0, 1, 1, 2)
K_SLOTS = (0, 1, 2, 0, 1, 0)
SROWS = len(Q_SLOTS) * HD
GUARD = 3
KROWS = SROWS + GUARD
MASKED = -1.0e38

VA_W = 64
VB_ONE = 1 + 2 * HD
VB_W = 2 * VB_ONE + VA_W
VB_M = VA_W + VB_ONE

ROUTED = 2 * T // CH + E
ROWS = (NCH + ROUTED) * CH
NEC = NCH + ROUTED
W13 = KT * 2 * 2 * F
W2 = KT * D
WM = W13 + W2
FB = 2 * F // P
WROW = WM + 2 * FB + D

F32 = mybir.dt.float32
F32R = mybir.dt.float32r
BF16 = mybir.dt.bfloat16
I32 = mybir.dt.int32
U32 = mybir.dt.uint32
ALU = mybir.AluOpType
ACT = mybir.ActivationFunctionType
AX_X = mybir.AxisListType.X

assert NEC % 2 == 0 and ROUTED * CH % (P * B * PAIRS // 2) == 0


class Phase:

    def __init__(self, nc, ctx, name):
        self.nc, self.ctx, self.name = nc, ctx, name
        self.sems = []
        ctx.callback(self.end)

    def end(self):
        if self.sems:
            self.nc.clear_and_free_semaphores(self.sems)
            self.nc.all_engine_barrier()

    def sb(self, name, shape, dt=F32):
        return self.ctx.enter_context(self.nc.sbuf_tensor(f"{self.name}_{name}", shape, dt))

    def sb2(self, name, shape, dt=F32):
        return [self.sb(f"{name}{s}", shape, dt) for s in range(2)]

    def ps(self, name, shape):
        return self.ctx.enter_context(self.nc.psum_tensor(f"{self.name}_{name}", shape, F32))

    def sem(self, name):
        self.sems.append(self.nc.alloc_semaphore(f"{self.name}_{name}"))
        return self.sems[-1]

    def sem2(self, name):
        return [self.sem(f"{name}{s}") for s in range(2)]


def in_steps(eng, count, step):
    def chunk(n, s):
        def at(d):
            m, t = n + (s + d) // 2, (s + d) % 2
            if isinstance(n, int) and not 0 <= 2 * m + t < count:
                return None
            return m, t
        return at

    half = count // 2
    for j in range(3):
        step(chunk(j // 2, j % 2))
    with eng.Fori(1, half - 2) as it:
        step(chunk(it, 1))
        step(chunk(it + 1, 0))
    for j in range(count - 3, count):
        step(chunk(j // 2, j % 2))


def in_pairs(eng, count, step):
    in_steps(eng, count, lambda at: step(*at(0), at(1), at(-1)))


def in_rounds(eng, count, round_):
    round_(0)
    with eng.Fori(1, count) as it:
        round_(it)


def chunk_of(n, s):
    return bass.ds(n * 2 + s, 1)


def bcast(ap, at, shape):
    return ap.unsqueeze(at).broadcast_to(shape)


def build(nc, x, w_q, w_k, w_v, w_o, b_o, gate_w, gate_b, w1, b1, w3, b3, w2, b2,
          sw1, sb1, sw3, sb3, sw2, sb2, out):
    def dram(name, shape, dt=F32):
        return nc.dram_tensor(name, shape, dt, kind="Internal").ap()

    qk_parts = dram("qk_parts", (NCH, 2, 3, D, CH), BF16)
    va_scr = dram("va_scr", (NCH, PAIRS, P, TPC * 2 * VA_W), BF16)
    guard = dram("guard", (B, PAIRS, GUARD, 2, SEQ), BF16)
    ctx_scr = dram("ctx_scr", (T, D))
    x1_scr = dram("x1_scr", (NCH, P, TPC, D))
    rows_in = dram("rows_in", (ROWS, D))
    rows_out = dram("rows_out", (ROWS, D))
    w_scr = dram("w_scr", (E + 1, P, WROW))

    x_ch = x.rearrange("b (c j p) d -> (b c) p j d", j=TPC, p=P)
    out_ch = out.rearrange("b (c j p) d -> (b c) p j d", j=TPC, p=P)
    ctx_ch = ctx_scr.rearrange("(c j p) d -> c p j d", j=TPC, p=P)
    rin_ch = rows_in.rearrange("(c j p) d -> c p j d", j=TPC, p=P)
    rout_ch = rows_out.rearrange("(c j p) d -> c p j d", j=TPC, p=P)

    with ExitStack() as whole:
        keep = Phase(nc, whole, "keep")
        ident = keep.sb("ident", [P, P])
        power = keep.sb("power", [P, TPC])
        minus_one = keep.sb("minus_one", [P, TPC])
        heads_of = keep.sb("heads_of", [P, 4, 2 * H], BF16)
        norms = keep.sb("norms", [2 * H, NCH])
        wqkv = [keep.sb(f"wqkv_{h}", [P, KT, 3 * D], F32R) for h in ("hi", "lo")]
        wo = [keep.sb(f"wo_{h}", [P, KT, D], F32R) for h in ("hi", "lo")]
        gw = [keep.sb(f"gw_{h}", [P, KT, E], F32R) for h in ("hi", "lo")]
        logits = keep.sb("logits", [E, T])
        weight = keep.sb("weight", [P, 2, NT])
        slot = keep.sb("slot", [P, 2, NT], I32)
        expert_of = keep.sb("expert_of", [1, NEC], I32)

        prepare_weights(nc, ident, power, minus_one, heads_of, wqkv, wo, gw, w_q, w_k, w_v, w_o, gate_w,
                        w1, b1, w3, b3, w2, b2, sw1, sb1, sw3, sb3, sw2, sb2, w_scr, guard)
        project(nc, ident, power, minus_one, heads_of, norms, wqkv, x_ch, qk_parts, va_scr)
        find_maxima(nc, ident, norms, qk_parts, guard)
        attend(nc, ident, qk_parts, va_scr, guard, ctx_ch, rows_in)
        attention_out(nc, ident, power, minus_one, wo, gw, b_o, x_ch, ctx_ch, x1_scr, rin_ch, logits)
        route(nc, ident, gate_b, logits, weight, slot, expert_of)
        experts(nc, ident, rin_ch, rows_in, rout_ch, w_scr, slot, expert_of)
        combine(nc, power, rout_ch, rows_out, x1_scr, weight, slot, out_ch)


def prepare_weights(nc, ident, power, minus_one, heads_of, wqkv, wo, gw, w_q, w_k, w_v, w_o, gate_w,
                    w1, b1, w3, b3, w2, b2, sw1, sb1, sw3, sb3, sw2, sb2, w_scr, guard):
    with ExitStack() as ctx:
        ph = Phase(nc, ctx, "prep")
        raw = ph.sb("raw", [P, 4, KT, D])
        graw = ph.sb("graw", [E, D])
        zeros = ph.sb("zeros", [P, SEQ // 2])
        ein = ph.sb2("ein", [P, 2 * FB + KT, D])
        eout = ph.sb2("eout", [P, WROW])
        pt = [ph.ps(f"pt{i}", [P, KT * D]) for i in range(3)]
        pe5 = [ph.ps(f"pe{i}", [P, CH]) for i in range(5)]
        made = ph.sem("constants_made")
        iz = ph.sem("identity_zeroed")
        loaded = ph.sem("weights_loaded")
        turned = ph.sem("weights_transposed")
        hi_done = ph.sem("hi_done")
        lo_done = ph.sem("lo_done")
        zeroed = ph.sem("scratch_zeroed")
        e_loaded = ph.sem2("expert_loaded")
        e_turned = ph.sem("expert_bank_transposed")
        e_copied_a = ph.sem("expert_bank_copied_by_scalar")
        e_copied_v = ph.sem("expert_bank_copied_by_vector")
        e_stored = ph.sem2("expert_stored")
        dst = [(wqkv, 0), (wqkv, 1), (wqkv, 2), (wo, 0)]

        def half(pair, which, m):
            buf, at = pair
            return buf[which][:, :, at * D:(at + 1) * D]

        def sources(e):
            if e is None:
                return sw1, sb1, sw3, sb3, sw2, sb2
            pick = lambda w: w[bass.ds(e, 1)].rearrange(
                "a r c -> (a r) c" if len(w.shape) == 3 else "a r -> (a r)")
            return tuple(pick(w) for w in (w1, b1, w3, b3, w2, b2))

        with nc.Block() as block:
            @block.gpsimd
            def _(pool):
                nc.gpsimd.memset(ident[:], 0.0).then_inc(iz, 1)
                nc.gpsimd.memset(power[:], -0.5).then_inc(made, 1)
                nc.gpsimd.memset(minus_one[:], -1.0).then_inc(made, 1)
                nc.gpsimd.memset(zeros[:], 0.0).then_inc(made, 1)
                nc.gpsimd.memset(heads_of[:], 0.0).then_inc(iz, 1)
                pool.wait_ge(iz, 2)
                nc.gpsimd.affine_select(out=ident[:], in_=ident[:], compare_op=ALU.not_equal, fill=1.0,
                                        base=0, pattern=[[-1, P]], channel_multiplier=1).then_inc(made, 1)
                for m in range(4):
                    at = m * (P // HD)
                    own = heads_of[:, m, at:at + P // HD]
                    nc.gpsimd.memset(own, 1.0).then_inc(iz, 1)
                    pool.wait_ge(iz, 3 + 3 * m)
                    nc.gpsimd.affine_select(out=own, in_=own, compare_op=ALU.is_ge, fill=0.0, base=0,
                                            pattern=[[-HD, P // HD]], channel_multiplier=1).then_inc(iz, 1)
                    pool.wait_ge(iz, 4 + 3 * m)
                    nc.gpsimd.affine_select(out=own, in_=own, compare_op=ALU.is_ge, fill=0.0, base=HD - 1,
                                            pattern=[[HD, P // HD]], channel_multiplier=-1).then_inc(iz, 1)
                pool.wait_ge(iz, 2 + 3 * 4)
                pool.wait_ge(made, 4)
                rows = B * PAIRS * GUARD
                pool.dma_start(guard.rearrange("b q g h t -> (b q g) h t"),
                               bcast(zeros[0:rows, :].bitcast(BF16), 1, [rows, 2, SEQ])).then_inc(zeroed, 16)
                pool.wait_ge(zeroed, 16)

            @block.sync
            def _(sp):
                for m, w in enumerate((w_q, w_k, w_v, w_o)):
                    sp.dma_start(raw[:, m], w.rearrange("(o p) i -> p o i", p=P)).then_inc(loaded, 16)
                sp.dma_start(graw[:], gate_w).then_inc(loaded, 16)

                def load(e, n, s):
                    a1, c1, a3, c3, a2, c2 = sources(e)
                    sp.wait_ge(e_stored[s], n * 16)
                    for i, w in enumerate((a1, a3)):
                        for par in range(2):
                            sp.dma_start(ein[s][:, i * FB + 2 * par:i * FB + 2 * par + 2, :],
                                         w.rearrange("(o p two) d -> two p o d", p=P, two=2)[par])\
                                .then_inc(e_loaded[s], 16)
                    sp.dma_start(ein[s][:, 2 * FB:, :], a2.rearrange("(o p) f -> p o f", p=P))\
                        .then_inc(e_loaded[s], 16)
                    for i, c in enumerate((c1, c3)):
                        for par in range(2):
                            with nc.allow_non_contiguous_dma(reason="a few biases, one to a partition"):
                                sp.dma_start(eout[s][:, WM + i * FB + 2 * par:WM + i * FB + 2 * par + 2],
                                             c.rearrange("(o p two) -> two p o", p=P, two=2)[par])\
                                    .then_inc(e_loaded[s], 16)
                    sp.dma_start(eout[s][:, WM + 2 * FB:], bcast(c2, 0, [P, D])).then_inc(e_loaded[s], 16)

                in_rounds(sp, E // 2, lambda it: [load(it * 2 + s, it, s) for s in range(2)])
                load(None, E // 2, 0)
                sp.wait_ge(e_stored[0], 16 * (E // 2 + 1))
                sp.wait_ge(e_stored[1], 16 * (E // 2))

            @block.tensor
            def _(pe):
                pe.wait_ge(made, 4)
                for m in range(4):
                    pe.wait_ge(loaded, 16 * 5)
                    if m >= 3:
                        pe.wait_ge(lo_done, m - 2)
                    for k in range(KT):
                        for o in range(KT):
                            last = nc.tensor.transpose(pt[m % 3][:, k * D + o * P:k * D + (o + 1) * P],
                                                       raw[:, m, o, k * P:(k + 1) * P], ident[:])
                    last.then_inc(turned, 1)
                pe.wait_ge(lo_done, 2)
                for k in range(KT):
                    last = nc.tensor.transpose(pt[1][:, k * E:(k + 1) * E], graw[:, k * P:(k + 1) * P],
                                               ident[0:E, 0:E])
                last.then_inc(turned, 1)

                def turn(n, s, banks):
                    pe.wait_ge(e_loaded[s], (n + 1) * 160)
                    for i in range(5):
                        if i < 2 or i == 4:
                            pe.wait_ge(e_copied_a, banks[0])
                        else:
                            pe.wait_ge(e_copied_v, banks[1])
                        if i < 4:
                            w, k = i // 2, i % 2
                            for o in range(FB):
                                last = nc.tensor.transpose(pe5[i][:, o * P:(o + 1) * P],
                                                           ein[s][:, w * FB + o, k * P:(k + 1) * P], ident[:])
                        else:
                            for k in range(KT):
                                for o in range(KT):
                                    last = nc.tensor.transpose(
                                        pe5[i][:, k * D + o * P:k * D + (o + 1) * P],
                                        ein[s][:, 2 * FB + o, k * P:(k + 1) * P], ident[:])
                        last.then_inc(e_turned, 1)

                in_rounds(pe, E // 2, lambda it: [turn(it, s, ((it * 2 + s) * 3, (it * 2 + s) * 2)) for s in range(2)])
                turn(E // 2, 0, (E * 3, E * 2))

            @block.scalar
            def _(act):
                for m in range(4):
                    act.wait_ge(turned, m + 1)
                    nc.scalar.activation(half(dst[m], 0, m), pt[m % 3][:].rearrange("p (k o) -> p k o", k=KT),
                                         ACT.Copy).then_inc(hi_done, 1)
                act.wait_ge(turned, 5)
                nc.scalar.activation(gw[0][:], pt[1][:, 0:KT * E].rearrange("p (k o) -> p k o", k=KT),
                                     ACT.Copy).then_inc(hi_done, 1)

                def copy(e, n, s, k):
                    act.wait_ge(e_stored[s], n * 16)
                    for i, at in ((0, 0), (1, 2 * F), (4, W13)):
                        act.wait_ge(e_turned, k * 5 + i + 1)
                        nc.scalar.activation(eout[s][:, at:at + CH], pe5[i][:], ACT.Copy)\
                            .then_inc(e_copied_a, 1)
                    act.wait_ge(e_copied_a, k * 3 + 3)
                    act.wait_ge(e_copied_v, k * 2 + 2)
                    act.wait_ge(e_loaded[s], (n + 1) * 160)
                    act.dma_start(w_scr[bass.ds(e, 1)].rearrange("a p w -> (a p) w"), eout[s][:])\
                        .then_inc(e_stored[s], 16)

                in_rounds(act, E // 2, lambda it: [copy(it * 2 + s, it, s, it * 2 + s) for s in range(2)])
                copy(E, E // 2, 0, E)

            @block.vector
            def _(dve):
                for m in range(4):
                    dve.wait_ge(hi_done, m + 1)
                    nc.vector.tensor_tensor(half(dst[m], 1, m), pt[m % 3][:].rearrange("p (k o) -> p k o", k=KT),
                                            half(dst[m], 0, m).bitcast(F32), ALU.subtract).then_inc(lo_done, 1)
                dve.wait_ge(hi_done, 5)
                nc.vector.tensor_tensor(gw[1][:], pt[1][:, 0:KT * E].rearrange("p (k o) -> p k o", k=KT),
                                        gw[0][:].bitcast(F32), ALU.subtract).then_inc(lo_done, 1)

                def copy(n, s, k):
                    dve.wait_ge(e_stored[s], n * 16)
                    for i in (2, 3):
                        dve.wait_ge(e_turned, k * 5 + i + 1)
                        nc.vector.tensor_copy(eout[s][:, i * CH:(i + 1) * CH], pe5[i][:])\
                            .then_inc(e_copied_v, 1)

                in_rounds(dve, E // 2, lambda it: [copy(it, s, it * 2 + s) for s in range(2)])
                copy(E // 2, 0, E)


def stats_of(nc, dve, src, stats, mv, n, s, stats_done, stats_seen, mv_done):
    for j in range(TPC):
        nc.vector.bn_stats(stats[:, j], src[:, j]).then_inc(stats_done[s], 1)
    dve.wait_ge(stats_done[s], (n + 1) * TPC)
    dve.sem_inc(stats_seen, 1)
    for j in range(TPC):
        nc.vector.bn_aggr(mv[:, j], stats[:, j]).then_inc(mv_done[s], 1)


def inverse_roots(nc, pool, power, s, mv, std, rstd, mv_done, mv_seen, std_done, rstd_done, k):
    pool.wait_ge(mv_done[s], (k + 1) * TPC)
    pool.sem_inc(mv_seen, 1)
    nc.gpsimd.tensor_scalar(std[s][:], mv[s][:, :, 1], EPS, None, ALU.add).then_inc(std_done[s], 1)
    pool.wait_ge(std_done[s], k + 1)
    nc.gpsimd.tensor_tensor(rstd[s][:], std[s][:], power[:], ALU.pow).then_inc(rstd_done[s], 1)


def offsets(nc, pool, minus_one, s, mv, negated, rstd, shift, negated_done, rstd_done, shift_done, k):
    nc.gpsimd.tensor_tensor(negated[s][:], mv[s][:, :, 0], minus_one[:], ALU.mult).then_inc(negated_done[s], 1)
    pool.wait_ge(negated_done[s], k + 1)
    pool.wait_ge(rstd_done[s], k + 1)
    nc.gpsimd.tensor_tensor(shift[s][:], negated[s][:], rstd[s][:], ALU.mult).then_inc(shift_done[s], 1)


def transposes(nc, psum, src, ident):
    for k in range(KT):
        for j in range(TPC):
            last = nc.tensor.transpose(psum[:, k, j * P:(j + 1) * P], src[:, j, k * P:(k + 1) * P], ident[:])
    return last


PARTS3 = ((0, 0), (0, 1), (1, 0))


def product(nc, psum, left, right, lsl, rsl):
    steps = [(k, a, b) for k in range(KT) for a, b in PARTS3]
    for i, (k, a, b) in enumerate(steps):
        last = nc.tensor.matmul(psum, left[a][:, k, lsl], right[b][:, k, rsl],
                                start=(i == 0), stop=(i == len(steps) - 1))
    return last


def project(nc, ident, power, minus_one, heads_of, norms, wqkv, x_ch, qk_parts, va_scr):
    with ExitStack() as ctx:
        ph = Phase(nc, ctx, "proj")
        xin = ph.sb2("xin", [P, TPC, D])
        xn = ph.sb2("xn", [P, TPC, D])
        stats = ph.sb2("stats", [P, TPC, 6])
        mv = ph.sb2("mv", [P, TPC, 2])
        std = ph.sb2("std", [P, TPC])
        rstd = ph.sb2("rstd", [P, TPC])
        negated = ph.sb2("negated", [P, TPC])
        shift = ph.sb2("shift", [P, TPC])
        xt = [[ph.sb(f"xt{s}_{h}", [P, KT, CH], F32R) for h in ("hi", "lo")] for s in range(2)]
        qk = ph.sb2("qk", [P, 3, 4, CH], BF16)
        square = ph.sb("square", [P, 4, CH], BF16)
        rest = ph.sb2("rest", [P, 2, CH])
        va = ph.sb2("va", [P, PAIRS, TPC, 2, VA_W], BF16)
        vrest = ph.sb("vrest", [P, 2, PAIRS, TPC, HD])
        psT = ph.ps("psT", [P, KT, CH])
        psP = [ph.ps(f"psP{i}", [P, 2 * CH]) for i in range(3)]
        cleared = ph.sem("values_cleared")
        x_loaded, x_normed = ph.sem2("x_loaded"), ph.sem2("x_normed")
        stats_done, mv_done = ph.sem2("stats_done"), ph.sem2("mv_done")
        stats_seen, mv_seen = ph.sem("stats_seen"), ph.sem("mv_seen")
        std_done, rstd_done = ph.sem2("std_done"), ph.sem2("rstd_done")
        negated_done, shift_done = ph.sem2("negated_done"), ph.sem2("shift_done")
        turned, xt_done, lo_done = ph.sem2("x_turned"), ph.sem2("xt_hi_done"), ph.sem2("xt_lo_done")
        q_done, v_done = ph.sem2("qk_product_done"), ph.sem2("v_product_done")
        q1, qr1, q2, q3 = (ph.sem2(f"q_{n}") for n in ("part1", "rest1", "part2", "part3"))
        v1, vr1, v2, v3 = (ph.sem2(f"v_{n}") for n in ("part1", "rest1", "part2", "part3"))
        squared, summed, bounded = ph.sem2("squared"), ph.sem2("norms_summed"), ph.sem2("norms_bounded")
        qk_stored, v_stored = ph.sem2("qk_stored"), ph.sem2("v_stored")

        def v_psum(h):
            return psP[2][:].rearrange("p (j q h d) -> p h q j d", j=TPC, q=PAIRS, h=2)[:, h]

        def va_part(s, h, part):
            return va[s][:, :, :, h, 1 + part * HD:1 + (part + 1) * HD]

        def after(n):
            return not (isinstance(n, int) and n == NCH // 2 - 1)

        with nc.Block() as block:
            @block.sync
            def _(sp):
                def load(n, s):
                    sp.wait_ge(x_normed[s], n * TPC)
                    sp.dma_start(xin[s][:], x_ch[chunk_of(n, s)].rearrange("a p j d -> p (a j) d"))\
                        .then_inc(x_loaded[s], 16)

                def step(at):
                    n, s = at(0)
                    if not at(-1):
                        load(0, 0)
                        load(0, 1)
                        load(1, 0)
                    if at(3):
                        load(*at(3))
                    sp.wait_ge(q3[s], n * 2 + 2)
                    for side in range(2):
                        for part in range(3):
                            sp.dma_start(
                                qk_parts[chunk_of(n, s), side, part].rearrange("a (h r) t -> r (a h) t", r=P),
                                qk[s][:, part, 2 * side:2 * side + 2, :]).then_inc(qk_stored[s], 16)
                    sp.wait_ge(v3[s], n * 2 + 2)
                    sp.dma_start(va_scr[chunk_of(n, s)].rearrange("a q p w -> p (a q) w"),
                                 va[s][:].rearrange("p q j h w -> p q (j h w)")).then_inc(v_stored[s], 16)

                in_steps(sp, NCH, step)
                for s in range(2):
                    sp.wait_ge(qk_stored[s], NCH // 2 * 96)
                    sp.wait_ge(v_stored[s], NCH // 2 * 16)

            @block.gpsimd
            def _(pool):
                for s in range(2):
                    nc.gpsimd.memset(va[s][:].bitcast(F32), 0.0).then_inc(cleared, 1)
                pool.wait_ge(cleared, 2)
                for s in range(2):
                    nc.gpsimd.memset(va[s][:, :, :, :, 0:1], 1.0).then_inc(cleared, 1)

                def step(n, s, nxt, prv):
                    inverse_roots(nc, pool, power, s, mv, std, rstd, mv_done, mv_seen, std_done, rstd_done, n)
                    offsets(nc, pool, minus_one, s, mv, negated, rstd, shift, negated_done, rstd_done, shift_done, n)

                in_pairs(pool, NCH, step)

            @block.tensor
            def _(pe):
                def turn(n, s):
                    pe.wait_ge(x_normed[s], n * TPC + TPC)
                    if s == 1:
                        pe.wait_ge(lo_done[0], n + 1)
                        pe.wait_ge(bounded[1], n)
                    else:
                        pe.wait_ge(lo_done[1], n)
                        pe.wait_ge(bounded[0], n)
                    transposes(nc, psT, xn[s], ident).then_inc(turned[s], 1)

                def step(n, s, nxt, prv):
                    if prv is None:
                        turn(0, 0)
                    pe.wait_ge(lo_done[s], n + 1)
                    for side in range(2):
                        if s == 1:
                            pe.wait_ge(squared[0], n * 2 + side + 1)
                        else:
                            pe.wait_ge(squared[1], n * 2)
                        for m in range(2):
                            at = (2 * side + m) * P
                            last = product(nc, psP[side][:, m * CH:(m + 1) * CH], wqkv, xt[s],
                                           slice(at, at + P), slice(0, CH))
                        last.then_inc(q_done[s], 1)
                    if nxt is not None:
                        turn(*nxt)
                    if s == 1:
                        pe.wait_ge(vr1[0], n * 2 + 2)
                    else:
                        pe.wait_ge(vr1[1], n * 2)
                    for j in range(TPC):
                        last = product(nc, psP[2][:, j * D:(j + 1) * D], xt[s], wqkv, slice(j * P, (j + 1) * P),
                                       slice(2 * D, 3 * D))
                    last.then_inc(v_done[s], 1)
                    if nxt is not None:
                        pe.wait_ge(lo_done[nxt[1]], nxt[0] + 1)
                    else:
                        pe.wait_ge(bounded[prv[1]], prv[0] + 1)
                    pe.wait_ge(squared[s], n * 2 + 2)
                    for m in range(4):
                        last = nc.tensor.matmul(psT[0:2 * H, 0, :], heads_of[:, m], square[:, m],
                                                start=(m == 0), stop=(m == 3))
                    last.then_inc(summed[s], 1)

                in_pairs(pe, NCH, step)

            @block.scalar
            def _(act):
                def hi(n, s):
                    act.wait_ge(turned[s], n + 1)
                    nc.scalar.activation(xt[s][0][:], psT[:], ACT.Copy).then_inc(xt_done[s], 1)

                def normalize(n, s):
                    act.wait_ge(shift_done[s], n + 1)
                    act.wait_ge(turned[s], n)
                    for j in range(TPC):
                        nc.scalar.activation(xn[s][:, j], xin[s][:, j], ACT.Identity, bias=shift[s][:, j:j + 1],
                                             scale=rstd[s][:, j:j + 1]).then_inc(x_normed[s], 1)

                def step(n, s, nxt, prv):
                    if prv is None:
                        normalize(0, 0)
                        hi(0, 0)
                    if nxt is not None:
                        normalize(*nxt)
                    act.wait_ge(qk_stored[s], n * 96)
                    prod = [psP[side][:].rearrange("p (m t) -> p m t", m=2) for side in range(2)]
                    for side in range(2):
                        act.wait_ge(q_done[s], n * 2 + side + 1)
                        nc.scalar.activation(qk[s][:, 0, 2 * side:2 * side + 2], prod[side], ACT.Copy)\
                            .then_inc(q1[s], 1)
                    if nxt is not None:
                        hi(*nxt)
                    if prv is not None:
                        act.wait_ge(summed[prv[1]], prv[0] + 1)
                    for side in range(2):
                        act.wait_ge(qr1[s], n * 2 + side + 1)
                        nc.scalar.activation(square[:, 2 * side:2 * side + 2], prod[side], ACT.Square)\
                            .then_inc(squared[s], 1)
                        nc.scalar.activation(qk[s][:, 1, 2 * side:2 * side + 2], rest[side][:], ACT.Copy)\
                            .then_inc(q2[s], 1)
                    act.wait_ge(v_stored[s], n * 16)
                    act.wait_ge(cleared, 4)
                    act.wait_ge(v_done[s], n + 1)
                    for h in range(2):
                        nc.scalar.activation(va_part(s, h, 0), v_psum(h), ACT.Copy).then_inc(v1[s], 1)
                    for h in range(2):
                        act.wait_ge(vr1[s], n * 2 + h + 1)
                        nc.scalar.activation(va_part(s, h, 1), vrest[:, h], ACT.Copy).then_inc(v2[s], 1)

                in_pairs(act, NCH, step)

            @block.vector
            def _(dve):
                V = nc.vector

                def measure(n, s):
                    dve.wait_ge(x_loaded[s], n * 16 + 16)
                    dve.wait_ge(shift_done[s], n)
                    stats_of(nc, dve, xin[s], stats[s], mv[s], n, s, stats_done, stats_seen, mv_done)

                def lo(n, s):
                    dve.wait_ge(xt_done[s], n + 1)
                    V.tensor_tensor(xt[s][1][:], psT[:], xt[s][0][:].bitcast(F32), ALU.subtract)\
                        .then_inc(lo_done[s], 1)

                def bound(n, s):
                    dve.wait_ge(summed[s], n + 1)
                    V.tensor_reduce(norms[:, bass.ds(n * 2 + s, 1)], psT[0:2 * H, 0, :], AX_X, ALU.max)\
                        .then_inc(bounded[s], 1)

                def step(n, s, nxt, prv):
                    if prv is None:
                        measure(0, 0)
                        lo(0, 0)
                        measure(0, 1)
                    if prv is not None:
                        bound(*prv)
                    for side in range(2):
                        dve.wait_ge(q1[s], n * 2 + side + 1)
                        V.tensor_tensor(rest[side][:], psP[side][:].rearrange("p (m t) -> p m t", m=2),
                                        qk[s][:, 0, 2 * side:2 * side + 2], ALU.subtract).then_inc(qr1[s], 1)
                    if nxt is not None:
                        lo(*nxt)
                    if after(n):
                        measure(n + 1, s)
                    for side in range(2):
                        dve.wait_ge(q2[s], n * 2 + side + 1)
                        V.tensor_tensor(qk[s][:, 2, 2 * side:2 * side + 2], rest[side][:],
                                        qk[s][:, 1, 2 * side:2 * side + 2], ALU.subtract).then_inc(q3[s], 1)
                    dve.wait_ge(v1[s], n * 2 + 2)
                    for h in range(2):
                        V.tensor_tensor(vrest[:, h], v_psum(h), va_part(s, h, 0), ALU.subtract).then_inc(vr1[s], 1)
                    for h in range(2):
                        dve.wait_ge(v2[s], n * 2 + h + 1)
                        V.tensor_tensor(va_part(s, h, 2), vrest[:, h], va_part(s, h, 1), ALU.subtract)\
                            .then_inc(v3[s], 1)
                    if nxt is None:
                        bound(n, s)

                in_pairs(dve, NCH, step)


SAFE = 40.0


def find_maxima(nc, ident, norms, qk_parts, guard):
    with ExitStack() as ctx:
        ph = Phase(nc, ctx, "max")
        greatest = ph.sb("greatest", [2 * H, 1])
        row = ph.sb("row", [1, 2 * H])
        bounds = ph.sb("bounds", [1, H])
        bound = ph.sb("bound", [1, 1])
        flagf = ph.sb("flagf", [1, 1])
        flag = ph.sb("flag", [1, 1], I32)
        qs = ph.sb("qs", [SROWS, SEQ], BF16)
        ks = ph.sb("ks", [SROWS, SEQ], BF16)
        identb = ph.sb("identb", [P, P], BF16)
        tri = ph.sb("tri", [P, P], BF16)
        pre = ph.sb("pre", [P, P], BF16)
        top = ph.sb("top", [P, SEQ // P])
        minus = ph.sb("minus", [P, SEQ // P])
        rest = ph.sb("rest", [SEQ // P, 2, P])
        part = ph.sb("part", [SEQ // P, GUARD, P], BF16)
        pss = ph.ps("scores", [P, SEQ])
        pst = ph.ps("turned", [P, P])
        zeroed, made = ph.sem("masks_zeroed"), ph.sem("masks_made")
        step, row_turned = ph.sem("bound_steps"), ph.sem("row_turned")
        loaded, scored, tops, negated = (ph.sem(n) for n in ("head_loaded", "scores_ready", "maxima", "negated"))
        minus_turned, cut, stored = (ph.sem(n) for n in ("maxima_turned", "parts_cut", "parts_stored"))
        HEADS = 2 * B * PAIRS
        QT = SEQ // P
        LOADS = 2 * len(Q_SLOTS)

        def all_heads(eng, head):
            needed = eng.value_load(flag[0:1, 0:1], min_val=0, max_val=1)
            with eng.If(needed > 0):
                with eng.Fori(0, B) as b:
                    with eng.Fori(0, PAIRS) as pair:
                        for h in range(2):
                            head(b, pair, h, b * H + pair * 2 + h)
                if eng is nc.scalar:
                    eng.wait_ge(stored, HEADS * 16 * GUARD + 1)

        with nc.Block() as block:
            @block.vector
            def _(dve):
                V = nc.vector
                V.tensor_reduce(greatest[:], norms[:], AX_X, ALU.max).then_inc(step, 1)
                dve.wait_ge(row_turned, 1)
                V.tensor_copy(row[:], pst[0:1, 0:2 * H]).then_inc(step, 1)
                dve.wait_ge(step, 2)
                V.tensor_tensor(bounds[:], row[:, 0:H], row[:, H:], ALU.mult).then_inc(step, 1)
                dve.wait_ge(step, 3)
                V.tensor_reduce(bound[:], bounds[:], AX_X, ALU.max).then_inc(step, 1)
                dve.wait_ge(step, 4)
                V.tensor_scalar(flagf[:], bound[:], SAFE * SAFE * HD, None, ALU.is_gt).then_inc(step, 1)
                dve.wait_ge(step, 5)
                V.tensor_copy(flag[:], flagf[:]).then_inc(step, 1)

            @block.tensor
            def _(pe):
                pe.wait_ge(step, 1)
                nc.tensor.transpose(pst[0:1, 0:2 * H], greatest[:], ident[0:2 * H, 0:2 * H]).then_inc(row_turned, 1)

            @block.gpsimd
            def _(pool):
                nc.gpsimd.memset(identb[:], 0.0).then_inc(zeroed, 1)
                nc.gpsimd.memset(tri[:], 0.0).then_inc(zeroed, 1)
                nc.gpsimd.memset(pre[:], 0.0).then_inc(zeroed, 1)
                pool.wait_ge(zeroed, 3)
                nc.gpsimd.affine_select(out=identb[:], in_=identb[:], compare_op=ALU.not_equal, fill=1.0,
                                        base=0, pattern=[[-1, P]], channel_multiplier=1).then_inc(made, 1)
                left = PREFIX - P
                nc.gpsimd.affine_select(out=tri[:], in_=tri[:], compare_op=ALU.is_ge, fill=MASKED,
                                        base=0, pattern=[[-1, P]], channel_multiplier=1).then_inc(made, 1)
                nc.gpsimd.affine_select(out=pre[:, left:], in_=pre[:, left:], compare_op=ALU.is_ge, fill=MASKED,
                                        base=-left, pattern=[[-1, P - left]], channel_multiplier=1)\
                    .then_inc(made, 1)

        with nc.Block() as block:
            @block.sync
            def _(sp):
                sp.sem_inc(stored, 1)

                def head(b, pair, h, n):
                    sp.wait_ge(scored, n * QT + 1)
                    for side, buf, slots in ((0, qs, Q_SLOTS), (1, ks, K_SLOTS)):
                        for i, p in enumerate(slots):
                            sp.dma_start(
                                buf[i * HD:(i + 1) * HD].rearrange("r (c t) -> r c t", c=BCH),
                                qk_parts[bass.ds(b * BCH, BCH), side, p, bass.ds(pair * 2 * HD + h * HD, HD), :]
                                .rearrange("c r t -> r c t")).then_inc(loaded, 16)

                all_heads(sp, head)

            @block.tensor
            def _(pe):
                pe.sem_inc(scored, 1)

                def head(b, pair, h, n):
                    pe.wait_ge(loaded, (n + 1) * 16 * LOADS)
                    for t in range(QT):
                        keys = max((t + 1) * P, PREFIX)
                        masked = (t + 1) * P > PREFIX
                        pe.wait_ge(tops, n * QT + t + 1)
                        for c in range(0, keys, CH):
                            end = min(c + CH, keys)
                            diagonal = masked and end == keys
                            last = nc.tensor.matmul(pss[:, c:end], qs[:, t * P:(t + 1) * P], ks[:, c:end],
                                                    start=True, stop=not diagonal)
                            if diagonal:
                                mask = pre if t * P < PREFIX else tri
                                last = nc.tensor.matmul(pss[:, keys - P:keys], identb[:], mask[:],
                                                        start=False, stop=True)
                        last.then_inc(scored, 1)
                    pe.wait_ge(negated, n + 1)
                    nc.tensor.transpose(pst[0:QT, :], minus[:], ident[:]).then_inc(minus_turned, 1)

                all_heads(pe, head)

            @block.vector
            def _(dve):
                V = nc.vector
                dve.sem_inc(tops, 1)

                def head(b, pair, h, n):
                    for t in range(QT):
                        keys = max((t + 1) * P, PREFIX)
                        dve.wait_ge(scored, n * QT + t + 2)
                        V.tensor_reduce(top[:, t:t + 1], pss[:, 0:keys], AX_X, ALU.max).then_inc(tops, 1)
                    dve.wait_ge(tops, n * QT + QT + 1)
                    V.tensor_scalar(minus[:], top[:], -1.0, None, ALU.mult).then_inc(negated, 1)
                    dve.wait_ge(minus_turned, n + 1)
                    dve.wait_ge(stored, n * 16 * GUARD + 1)
                    V.tensor_copy(part[:, 0], pst[0:QT, :]).then_inc(cut, 1)
                    dve.wait_ge(cut, n * 5 + 1)
                    V.tensor_tensor(rest[:, 0], pst[0:QT, :], part[:, 0], ALU.subtract).then_inc(cut, 1)
                    dve.wait_ge(cut, n * 5 + 2)
                    V.tensor_copy(part[:, 1], rest[:, 0]).then_inc(cut, 1)
                    dve.wait_ge(cut, n * 5 + 3)
                    V.tensor_tensor(rest[:, 1], rest[:, 0], part[:, 1], ALU.subtract).then_inc(cut, 1)
                    dve.wait_ge(cut, n * 5 + 4)
                    V.tensor_copy(part[:, 2], rest[:, 1]).then_inc(cut, 1)

                all_heads(dve, head)

            @block.scalar
            def _(act):
                def head(b, pair, h, n):
                    act.wait_ge(cut, n * 5 + 5)
                    for g in range(GUARD):
                        act.dma_start(guard[bass.ds(b, 1), bass.ds(pair, 1), g, h].rearrange(
                            "a q (t p) -> t (a q p)", p=P), part[:, g]).then_inc(stored, 16)

                all_heads(act, head)


def units():
    for c in range(BCH):
        diagonal = TPC * c
        for kt in range(diagonal):
            yield c, ((kt, 0, 0),), 0
        yield c, ((diagonal, 0, 0),), 0
        if c == 0:
            assert P < PREFIX < 2 * P
            yield c, ((1, 0, 0),), 0
            yield c, ((2, 2 * P, 2 * P), (3, 3 * P, P)), P
        else:
            yield c, ((diagonal + 1, P, P), (diagonal + 3, 3 * P, 0)), 0
            yield c, ((diagonal + 2, 2 * P, 2 * P),), 2 * P


UNITS = list(units())
LAST_UNIT = {c: max(i for i, u in enumerate(UNITS) if u[0] == c) for c in range(BCH)}
SBUFS = 3
PBUFS = 4
VALUES = 3
COPY = VALUES + 1
TURN = VALUES + 2
FINISH = VALUES + 2


def attend(nc, ident, qk_parts, va_scr, guard, ctx_ch, rows_in):
    with ExitStack() as ctx:
        ph = Phase(nc, ctx, "att")
        qs = ph.sb2("qs", [KROWS, 2, SEQ], BF16)
        ks = ph.sb2("ks", [KROWS, 2, SEQ], BF16)
        va = ph.sb2("va", [P, SEQ // P, 2 * VA_W], BF16)
        vb = ph.sb2("vb", [P, SEQ // P, VB_W], F32R)
        prob = [ph.sb(f"prob{i}", [P, 2, CH]) for i in range(PBUFS)]
        low = [ph.sb(f"low{i}", [P, 2, CH], F32R) for i in range(PBUFS)]
        osb = ph.sb2("osb", [P, CH])
        csum = ph.sb2("csum", [P, 2 * TPC, HD])
        rden = ph.sb2("rden", [P, 2 * TPC])
        cout = ph.sb2("cout", [P, TPC, 2 * HD])
        identb = ph.sb("identb", [P, P], BF16)
        tri = ph.sb("tri", [P, P], BF16)
        pre = ph.sb("pre", [P, 2, P], BF16)
        rounds = B * PAIRS // 2
        ZR = ROUTED * CH // P // rounds
        zeros = ph.sb("zeros", [P, ZR * D])
        vsum = [[ph.sb(f"vsum{s}_{h}", [P, SEQ // P, HD]) for h in range(2)] for s in range(2)]
        v_cleared = ph.sem("values_cleared")
        v_added, v_hi, v_less, v_cut = (ph.sem2(n) for n in ("two_parts_added", "values_hi", "less_hi", "values_cut"))
        z_made, z_stored = ph.sem("zeros_made"), ph.sem("zero_rows_stored")
        pss = [ph.ps(f"scores{i}", [P, 2, CH]) for i in range(SBUFS)]
        pso = [ph.ps(f"out{i}", [P, CH]) for i in range(2)]
        made, zeroed = ph.sem("masks_made"), ph.sem("masks_zeroed")
        loaded = ph.sem2("heads_loaded")
        scored, exped, lowed, used = (ph.sem(n) for n in ("scores_ready", "probs_ready", "low_ready", "probs_used"))
        o_copied, o_turned = ph.sem("out_copied"), ph.sem("out_turned")
        summed, inverted, c_done = ph.sem("parts_summed"), ph.sem("denominators_inverted"), ph.sem("context_done")
        stored = ph.sem2("context_stored")
        nu = len(UNITS)
        nb = 2 * nu
        nk = 2 * BCH
        LOADS = 4 * len(Q_SLOTS) + 2
        end_of = {s * nu + LAST_UNIT[c]: s * BCH + c for s in range(2) for c in range(BCH)}

        def stream(eng, work):
            def here(g, it, lag):
                u = g - lag
                if u < 0:
                    return None if isinstance(it, int) and it == 0 else (u + nb, it - 1)
                return (u, it)

            def round_(it):
                for g in range(nb):
                    work(lambda lag: here(g, it, lag))

            round_(0)
            with eng.Fori(1, rounds) as it:
                round_(it)
            for g in range(max(COPY, TURN, FINISH)):
                work(lambda lag: None if lag <= g else (nb + g - lag, rounds - 1))

        def so_far(it, per, more):
            return max(0, it * per + more) if isinstance(it, int) else it * per + more

        def ended(at):
            return (end_of[at[0]], at[1]) if at and at[0] in end_of else None

        with nc.Block() as block:
            @block.gpsimd
            def _(pool):
                nc.gpsimd.memset(identb[:], 0.0).then_inc(zeroed, 1)
                nc.gpsimd.memset(tri[:], 0.0).then_inc(zeroed, 1)
                nc.gpsimd.memset(pre[:], 0.0).then_inc(zeroed, 1)
                pool.wait_ge(zeroed, 3)
                nc.gpsimd.affine_select(out=identb[:], in_=identb[:], compare_op=ALU.not_equal, fill=1.0,
                                        base=0, pattern=[[-1, P]], channel_multiplier=1).then_inc(made, 1)
                nc.gpsimd.affine_select(out=tri[:], in_=tri[:], compare_op=ALU.is_ge, fill=MASKED,
                                        base=0, pattern=[[1, P]], channel_multiplier=-1).then_inc(made, 1)
                left = PREFIX - P
                nc.gpsimd.affine_select(out=pre[:, 0], in_=pre[:, 0], compare_op=ALU.is_gt, fill=MASKED,
                                        base=left, pattern=[[0, P]], channel_multiplier=-1).then_inc(made, 1)
                nc.gpsimd.affine_select(out=pre[:, 1, left:], in_=pre[:, 1, left:], compare_op=ALU.is_ge,
                                        fill=MASKED, base=left, pattern=[[1, P - left]],
                                        channel_multiplier=-1).then_inc(made, 1)
                nc.gpsimd.affine_select(out=pre[:, 1, 0:left], in_=pre[:, 1, 0:left], compare_op=ALU.is_gt,
                                        fill=MASKED, base=left, pattern=[[0, left]],
                                        channel_multiplier=-1).then_inc(made, 1)
                nc.gpsimd.memset(zeros[:], 0.0).then_inc(z_made, 1)
                for s in range(2):
                    nc.gpsimd.memset(vb[s][:].bitcast(F32), 0.0).then_inc(v_cleared, 1)
                pool.wait_ge(v_cleared, 2)
                for s in range(2):
                    for h in range(2):
                        at = h * (VB_ONE + VA_W)
                        nc.gpsimd.memset(vb[s][:, :, at:at + 1].bitcast(F32), 1.0).then_inc(v_cleared, 1)

                def divide(b, q, k, n):
                    s, c = k // BCH, k % BCH
                    pool.wait_ge(summed, n * nk + k + 1)
                    pool.wait_ge(inverted, n * nk + k + 1)
                    pool.wait_ge(stored[k % 2], (n * BCH + k // 2) * 16)
                    nc.gpsimd.tensor_tensor(cout[k % 2][:].rearrange("p j (h d) -> p (j h) d", h=2), csum[k % 2][:],
                                            rden[k % 2][:].unsqueeze(2).broadcast_to([P, 2 * TPC, HD]),
                                            ALU.mult).then_inc(c_done, 1)
                    pool.wait_ge(c_done, n * nk + k + 1)
                    pool.dma_start(
                        ctx_ch[bass.ds(b * BCH + c, 1), :, :, bass.ds((q * 2 + s) * 2 * HD, 2 * HD)]
                        .rearrange("a p j d -> p (a j) d"), cout[k % 2][:]).then_inc(stored[k % 2], 16)

                def cut_values(n, s):
                    pool.wait_ge(loaded[s], (n + 1) * 16 * LOADS)
                    pool.wait_ge(v_cut[s], n * 2)
                    part = lambda h, i: va[s][:, :, h * VA_W + 1 + i * HD:h * VA_W + 1 + (i + 1) * HD]
                    for h in range(2):
                        nc.gpsimd.tensor_tensor(vsum[s][h][:], part(h, 0), part(h, 1), ALU.add).then_inc(v_added[s], 1)
                    for h in range(2):
                        at = h * (VB_ONE + VA_W) + 1
                        pool.wait_ge(v_added[s], n * 2 + h + 1)
                        nc.gpsimd.tensor_tensor(vb[s][:, :, at:at + HD], vsum[s][h][:], part(h, 2), ALU.add)\
                            .then_inc(v_hi[s], 1)
                    for h in range(2):
                        at = h * (VB_ONE + VA_W) + 1
                        pool.wait_ge(v_hi[s], n * 2 + h + 1)
                        nc.gpsimd.tensor_tensor(vsum[s][h][:], vsum[s][h][:], vb[s][:, :, at:at + HD].bitcast(F32),
                                                ALU.subtract).then_inc(v_less[s], 1)
                    for h in range(2):
                        at = h * (VB_ONE + VA_W) + 1 + HD
                        pool.wait_ge(v_less[s], n * 2 + h + 1)
                        nc.gpsimd.tensor_tensor(vb[s][:, :, at:at + HD], vsum[s][h][:], part(h, 2), ALU.add)\
                            .then_inc(v_cut[s], 1)

                def round_(b, q, n, last=False):
                    for k in range(nk):
                        divide(b, q, k, n)
                        if k == 1:
                            cut_values(n, 1)
                        if k == nk - 3 and not last:
                            cut_values(n + 1, 0)

                half = PAIRS // 2
                cut_values(0, 0)
                round_(0, 0, 0)
                with pool.Fori(1, half) as q:
                    round_(0, q, q)
                with pool.Fori(1, B - 1) as b:
                    with pool.Fori(0, half) as q:
                        round_(b, q, b * half + q)
                with pool.Fori(0, half - 1) as q:
                    round_(B - 1, q, q + (B - 1) * half)
                round_(B - 1, half - 1, rounds - 1, last=True)
                for s in range(2):
                    pool.wait_ge(stored[s], rounds * BCH * 16)

            @block.sync
            def _(sp):
                def load(b, n, pair, s):
                    if not isinstance(n, int):
                        sp.wait_ge(used, (n - 1) * nb + (s + 1) * nu)
                    for side, buf, slots in ((0, qs, Q_SLOTS), (1, ks, K_SLOTS)):
                        for i, part in enumerate(slots):
                            for h in range(2):
                                sp.dma_start(
                                    buf[s][i * HD:(i + 1) * HD, h].rearrange("r (c t) -> r c t", c=BCH),
                                    qk_parts[bass.ds(b * BCH, BCH), side, part, bass.ds(pair * 2 * HD + h * HD, HD), :]
                                    .rearrange("c r t -> r c t")).then_inc(loaded[s], 16)
                    sp.dma_start(qs[s][SROWS:KROWS], guard[bass.ds(b, 1), bass.ds(pair, 1)].rearrange(
                        "a q g h t -> (a q g) h t")).then_inc(loaded[s], 16)
                    sp.dma_start(va[s][:].rearrange("p (c j) w -> p c (j w)", c=BCH),
                                 va_scr[bass.ds(b * BCH, BCH), bass.ds(pair, 1)].rearrange(
                                     "c q p w -> p (c q) w")).then_inc(loaded[s], 16)

                sorted_rows = rows_in[NCH * CH:, :].rearrange("(n p r) d -> n p (r d)", p=P, r=ZR)

                def zero_rows(n):
                    sp.dma_start(sorted_rows[bass.ds(n, 1)].rearrange("n p w -> p (n w)"), zeros[:])\
                        .then_inc(z_stored, 16)

                def batch(b, first):
                    with sp.Fori(first, PAIRS // 2) as q:
                        for s in range(2):
                            load(b, b * (PAIRS // 2) + q, q * 2 + s, s)
                        zero_rows(b * (PAIRS // 2) + q)

                for s in range(2):
                    load(0, 0, s, s)
                sp.wait_ge(z_made, 1)
                zero_rows(0)
                batch(0, 1)
                with sp.Fori(1, B) as b:
                    batch(b, 0)
                sp.wait_ge(z_stored, 16 * rounds)

            @block.tensor
            def _(pe):
                pe.wait_ge(made, 7)

                def scores(g, it):
                    s, i = divmod(g, nu)
                    c, blocks, _ = UNITS[i]
                    if i == 0:
                        pe.wait_ge(loaded[s], (it + 1) * 16 * LOADS)
                    pe.wait_ge(exped, so_far(it, nb, g - SBUFS + 1))
                    for h in range(2):
                        for kt, q0, at in blocks:
                            mask = None
                            if kt * P < PREFIX:
                                if c == 0 and (kt + 1) * P > PREFIX:
                                    mask, w = pre[:].rearrange("p a b -> p (a b)"), 2 * P
                            elif c * TPC <= kt:
                                mask, w = tri[:], P
                            out = pss[g % SBUFS][:, h, at:at + CH - q0]
                            last = nc.tensor.matmul(out, ks[s][:, h, kt * P:(kt + 1) * P],
                                                    qs[s][:, h, c * CH + q0:(c + 1) * CH],
                                                    start=True, stop=mask is None)
                            if mask is not None:
                                last = nc.tensor.matmul(out[:, 0:w], identb[:], mask, start=False, stop=True)
                    last.then_inc(scored, 1)

                def values(g, it):
                    s, i = divmod(g, nu)
                    c, blocks, _ = UNITS[i]
                    k = s * BCH + c
                    o = pso[k % 2]
                    pe.wait_ge(lowed, it * nb + g + 1)
                    if i == 0:
                        pe.wait_ge(v_cleared, 6)
                        pe.wait_ge(v_cut[s], (it + 1) * 2)
                    if blocks[0][0] == 0:
                        done = so_far(it, nk, k - 1)
                        pe.wait_ge(summed, done)
                        pe.wait_ge(inverted, done)
                    upper = prob[g % PBUFS][:].bitcast(BF16)
                    for h in range(2):
                        for kt, q0, at in blocks:
                            nc.tensor.matmul(o[h * VA_W:(h + 1) * VA_W, q0:], va[s][:, kt, h * VA_W:(h + 1) * VA_W],
                                             upper[:, h, 2 * at + 1:2 * (at + CH - q0):2], start=(kt == 0), stop=False,
                                             skip_group_check=True)
                    for h in range(2):
                        for kt, q0, at in blocks:
                            first = h * VB_ONE
                            last = nc.tensor.matmul(o[0:VB_M, q0:], vb[s][:, kt, first:first + VB_M],
                                                    low[g % PBUFS][:, h, at:at + CH - q0], start=False,
                                                    stop=(i == LAST_UNIT[c]), skip_group_check=True)
                    last.then_inc(used, 1)

                def turn(k, it):
                    pe.wait_ge(o_copied, it * nk + k + 1)
                    for j in range(TPC):
                        last = nc.tensor.transpose(pso[k % 2][:, j * P:(j + 1) * P],
                                                   osb[k % 2][:, j * P:(j + 1) * P], ident[:])
                    last.then_inc(o_turned, 1)

                def work(earlier):
                    if earlier(0):
                        scores(*earlier(0))
                    if earlier(VALUES):
                        values(*earlier(VALUES))
                    if ended(earlier(TURN)):
                        turn(*ended(earlier(TURN)))

                stream(pe, work)

            @block.scalar
            def _(act):
                def probabilities(g, it):
                    first = UNITS[g % nu][2]
                    act.wait_ge(scored, it * nb + g + 1)
                    act.wait_ge(used, so_far(it, nb, g - PBUFS + 1))
                    nc.scalar.activation(prob[g % PBUFS][:, :, first:], pss[g % SBUFS][:, :, first:],
                                         ACT.Exp, scale=HD ** -0.5).then_inc(exped, 1)

                def copy(k, it, e):
                    act.wait_ge(used, it * nb + e + 1)
                    act.wait_ge(o_turned, so_far(it, nk, k - 1))
                    nc.scalar.activation(osb[k % 2][:], pso[k % 2][:], ACT.Copy).then_inc(o_copied, 1)

                def work(earlier):
                    if earlier(0):
                        probabilities(*earlier(0))
                    if ended(earlier(COPY)):
                        copy(*ended(earlier(COPY)), earlier(COPY)[0])

                stream(act, work)

            @block.vector
            def _(dve):
                V = nc.vector
                for s in range(2):
                    V.memset(ks[s][SROWS:KROWS], 1.0).then_inc(made, 1)

                def rest(g, it):
                    first = UNITS[g % nu][2]
                    dve.wait_ge(exped, it * nb + g + 1)
                    dve.wait_ge(used, so_far(it, nb, g - PBUFS + 1))
                    V.tensor_tensor(low[g % PBUFS][:, :, first:], prob[g % PBUFS][:, :, first:],
                                    prob[g % PBUFS][:].bitcast(BF16)[:, :, 2 * first + 1:2 * CH:2],
                                    ALU.subtract).then_inc(lowed, 1)

                def finish(k, it):
                    dve.wait_ge(o_turned, it * nk + k + 1)
                    dve.wait_ge(c_done, so_far(it, nk, k - 1))
                    o = pso[k % 2][:].rearrange("p (g w) -> p g w", w=VA_W)
                    V.tensor_reduce(csum[k % 2][:], o[:, :, 1:1 + 3 * HD].rearrange(
                        "p g (a d) -> p g d a", a=3), AX_X, ALU.add).then_inc(summed, 1)
                    V.reciprocal(rden[k % 2][:], o[:, :, 0]).then_inc(inverted, 1)

                def work(earlier):
                    if earlier(0):
                        rest(*earlier(0))
                    if ended(earlier(FINISH)):
                        finish(*ended(earlier(FINISH)))

                stream(dve, work)


def attention_out(nc, ident, power, minus_one, wo, gw, b_o, x_ch, ctx_ch, x1_scr, rin_ch, logits):
    with ExitStack() as ctx:
        ph = Phase(nc, ctx, "out")
        cin = ph.sb2("cin", [P, TPC, D])
        xin = ph.sb2("xin", [P, TPC, D])
        att = ph.sb2("att", [P, TPC, D])
        an = ph.sb2("attn", [P, TPC, D])
        x1 = ph.sb2("x1", [P, TPC, D])
        xn = ph.sb2("xn", [P, TPC, D])
        bias = ph.sb("bias", [P, D])
        stats = [ph.sb2(f"stats{i}_", [P, TPC, 6]) for i in range(2)]
        mv = [ph.sb2(f"mv{i}_", [P, TPC, 2]) for i in range(2)]
        std = [ph.sb2(f"std{i}_", [P, TPC]) for i in range(2)]
        rstd = [ph.sb2(f"rstd{i}_", [P, TPC]) for i in range(2)]
        negated = [ph.sb2(f"negated{i}_", [P, TPC]) for i in range(2)]
        shift = [ph.sb2(f"shift{i}_", [P, TPC]) for i in range(2)]
        ct = [[ph.sb(f"ct{s}_{h}", [P, KT, CH], F32R) for h in ("hi", "lo")] for s in range(2)]
        nt = [[ph.sb(f"nt{s}_{h}", [P, KT, CH], F32R) for h in ("hi", "lo")] for s in range(2)]
        psT = ph.ps("psT", [P, KT, CH])
        psN = ph.ps("psN", [P, KT, CH])
        psO = [ph.ps(f"psO{i}", [P, 2, D]) for i in range(2)]
        psG = [ph.ps(f"psG{i}", [E, CH]) for i in range(2)]
        b_loaded = ph.sem("bias_loaded")
        c_loaded, x_loaded = ph.sem2("context_loaded"), ph.sem2("x_loaded")
        c_turned, c_hi, c_lo = ph.sem2("context_turned"), ph.sem2("context_hi"), ph.sem2("context_lo")
        n_turned, n_hi, n_lo = ph.sem2("normed_turned"), ph.sem2("normed_hi"), ph.sem2("normed_lo")
        o_done, biased = ph.sem2("projected"), ph.sem2("bias_added")
        stats_done = [ph.sem2(f"stats{i}_done") for i in range(2)]
        mv_done = [ph.sem2(f"mv{i}_done") for i in range(2)]
        stats_seen, mv_seen = ph.sem("stats_seen"), ph.sem("mv_seen")
        std_done = [ph.sem2(f"std{i}_done") for i in range(2)]
        rstd_done = [ph.sem2(f"rstd{i}_done") for i in range(2)]
        negated_done = [ph.sem2(f"negated{i}_done") for i in range(2)]
        shift_done = [ph.sem2(f"shift{i}_done") for i in range(2)]
        a_normed, x1_done, x_normed = ph.sem2("att_normed"), ph.sem2("x1_done"), ph.sem2("x1_normed")
        g_done, g_kept = ph.sem2("logits_done"), ph.sem2("logits_kept")
        x1_stored, xn_stored = ph.sem2("x1_stored"), ph.sem2("normed_stored")

        with nc.Block() as block:
            @block.sync
            def _(sp):
                sp.dma_start(bias[:], bcast(b_o, 0, [P, D])).then_inc(b_loaded, 16)

                def load_context(n, s):
                    sp.wait_ge(c_turned[s], n)
                    sp.dma_start(cin[s][:], ctx_ch[chunk_of(n, s)].rearrange("a p j d -> p (a j) d"))\
                        .then_inc(c_loaded[s], 16)

                def load_x(n, s):
                    sp.wait_ge(x1_done[s], n)
                    sp.dma_start(xin[s][:], x_ch[chunk_of(n, s)].rearrange("a p j d -> p (a j) d"))\
                        .then_inc(x_loaded[s], 16)

                def step(at):
                    n, s = at(0)
                    if not at(-1):
                        load_context(0, 0)
                        load_context(0, 1)
                        load_context(1, 0)
                        load_x(0, 0)
                    if at(3):
                        load_context(*at(3))
                    if at(1):
                        load_x(*at(1))
                    sp.wait_ge(x1_done[s], n + 1)
                    sp.dma_start(x1_scr[chunk_of(n, s)].rearrange("a p j d -> p (a j) d"), x1[s][:])\
                        .then_inc(x1_stored[s], 16)
                    sp.wait_ge(x_normed[s], (n + 1) * TPC)
                    sp.dma_start(rin_ch[chunk_of(n, s)].rearrange("a p j d -> p (a j) d"), xn[s][:])\
                        .then_inc(xn_stored[s], 16)

                in_steps(sp, NCH, step)
                for s in range(2):
                    sp.wait_ge(x1_stored[s], NCH // 2 * 16)
                    sp.wait_ge(xn_stored[s], NCH // 2 * 16)

            @block.gpsimd
            def _(pool):
                def roots(i, n, s):
                    inverse_roots(nc, pool, power, s, mv[i], std[i], rstd[i], mv_done[i], mv_seen, std_done[i],
                                  rstd_done[i], n)
                    offsets(nc, pool, minus_one, s, mv[i], negated[i], rstd[i], shift[i], negated_done[i],
                            rstd_done[i], shift_done[i], n)

                def step(at):
                    if not at(-1):
                        roots(0, 0, 0)
                    if at(1):
                        roots(0, *at(1))
                    roots(1, *at(0))

                in_steps(pool, NCH, step)

            @block.tensor
            def _(pe):
                def turn(n, s):
                    pe.wait_ge(c_loaded[s], n * 16 + 16)
                    if s == 1:
                        pe.wait_ge(c_lo[0], n + 1)
                    else:
                        pe.wait_ge(c_lo[1], n)
                    transposes(nc, psT, cin[s], ident).then_inc(c_turned[s], 1)

                def projection(n, s):
                    pe.wait_ge(c_lo[s], n + 1)
                    for t in range(2):
                        if s == 1:
                            pe.wait_ge(biased[0], n * 2 + t + 1)
                        else:
                            pe.wait_ge(biased[1], n * 2)
                        for u in range(2):
                            j = 2 * t + u
                            last = product(nc, psO[t][:, u], ct[s], wo, slice(j * P, (j + 1) * P), slice(0, D))
                        last.then_inc(o_done[s], 1)

                def turn_normed(n, s):
                    pe.wait_ge(x_normed[s], n * TPC + TPC)
                    if s == 1:
                        pe.wait_ge(n_lo[0], n + 1)
                    else:
                        pe.wait_ge(n_lo[1], n)
                    transposes(nc, psN, xn[s], ident).then_inc(n_turned[s], 1)

                def router(n, s):
                    pe.wait_ge(n_lo[s], n + 1)
                    pe.wait_ge(g_kept[s], n)
                    product(nc, psG[s][:], gw, nt[s], slice(0, E), slice(0, CH)).then_inc(g_done[s], 1)

                def step(at):
                    if not at(-1):
                        turn(0, 0)
                        projection(0, 0)
                        turn(0, 1)
                    if at(1):
                        projection(*at(1))
                    if at(2):
                        turn(*at(2))
                    if at(-2):
                        router(*at(-2))
                    if at(-1):
                        turn_normed(*at(-1))
                    if not at(1):
                        router(*at(-1))
                        turn_normed(*at(0))
                        router(*at(0))

                in_steps(pe, NCH, step)

            @block.scalar
            def _(act):
                def context_hi(n, s):
                    act.wait_ge(c_turned[s], n + 1)
                    nc.scalar.activation(ct[s][0][:], psT[:], ACT.Copy).then_inc(c_hi[s], 1)

                def normed_hi(n, s):
                    act.wait_ge(n_turned[s], n + 1)
                    nc.scalar.activation(nt[s][0][:], psN[:], ACT.Copy).then_inc(n_hi[s], 1)

                def keep_logits(n, s):
                    act.wait_ge(g_done[s], n + 1)
                    nc.scalar.activation(logits[:, bass.ds(n * (2 * CH) + s * CH, CH)], psG[s][:], ACT.Copy)\
                        .then_inc(g_kept[s], 1)

                def norm(i, n, s, src, dst, done):
                    act.wait_ge(shift_done[i][s], n + 1)
                    for j in range(TPC):
                        nc.scalar.activation(dst[:, j], src[:, j], ACT.Identity, bias=shift[i][s][:, j:j + 1],
                                             scale=rstd[i][s][:, j:j + 1]).then_inc(done[s], 1)

                def first_norm(n, s):
                    act.wait_ge(x1_done[s], n)
                    norm(0, n, s, att[s], an[s], a_normed)

                def second_norm(n, s):
                    act.wait_ge(xn_stored[s], n * 16)
                    act.wait_ge(n_turned[s], n)
                    norm(1, n, s, x1[s], xn[s], x_normed)

                def step(at):
                    if not at(-1):
                        context_hi(0, 0)
                        first_norm(0, 0)
                        context_hi(0, 1)
                    if at(2):
                        context_hi(*at(2))
                    if at(-2):
                        keep_logits(*at(-2))
                    if at(-1):
                        normed_hi(*at(-1))
                    if at(1):
                        first_norm(*at(1))
                    second_norm(*at(0))
                    if not at(1):
                        keep_logits(*at(-1))
                        normed_hi(*at(0))
                        keep_logits(*at(0))

                in_steps(act, NCH, step)

            @block.vector
            def _(dve):
                V = nc.vector
                dve.wait_ge(b_loaded, 16)

                def context_lo(n, s):
                    dve.wait_ge(c_hi[s], n + 1)
                    V.tensor_tensor(ct[s][1][:], psT[:], ct[s][0][:].bitcast(F32), ALU.subtract)\
                        .then_inc(c_lo[s], 1)

                def normed_lo(n, s):
                    dve.wait_ge(n_hi[s], n + 1)
                    V.tensor_tensor(nt[s][1][:], psN[:], nt[s][0][:].bitcast(F32), ALU.subtract)\
                        .then_inc(n_lo[s], 1)

                def measure(i, n, s, src):
                    stats_of(nc, dve, src, stats[i][s], mv[i][s], n, s, stats_done[i], stats_seen, mv_done[i])

                def add_bias(n, s):
                    dve.wait_ge(a_normed[s], n * TPC)
                    for t in range(2):
                        dve.wait_ge(o_done[s], n * 2 + t + 1)
                        V.tensor_tensor(att[s][:, 2 * t:2 * t + 2], psO[t][:],
                                        bcast(bias[:], 1, [P, 2, D]), ALU.add).then_inc(biased[s], 1)
                    dve.wait_ge(biased[s], n * 2 + 2)
                    measure(0, n, s, att[s])

                def residual(n, s):
                    dve.wait_ge(a_normed[s], (n + 1) * TPC)
                    dve.wait_ge(x_loaded[s], n * 16 + 16)
                    dve.wait_ge(x1_stored[s], n * 16)
                    dve.wait_ge(x_normed[s], n * TPC)
                    V.tensor_tensor(x1[s][:], an[s][:], xin[s][:], ALU.add).then_inc(x1_done[s], 1)
                    dve.wait_ge(x1_done[s], n + 1)
                    measure(1, n, s, x1[s])

                def step(at):
                    if not at(-1):
                        context_lo(0, 0)
                        add_bias(0, 0)
                        context_lo(0, 1)
                    if at(1):
                        add_bias(*at(1))
                    if at(2):
                        context_lo(*at(2))
                    residual(*at(0))
                    if at(-1):
                        normed_lo(*at(-1))
                    if not at(1):
                        normed_lo(*at(0))

                in_steps(dve, NCH, step)


def route(nc, ident, gate_b, logits, weight, slot, expert_of):
    with ExitStack() as ctx:
        ph = Phase(nc, ctx, "route")
        gb = ph.sb("gate_b", [P, E])
        top = ph.sb("top", [P, NT])
        ex = ph.sb("ex", [P, NT, E])
        den = ph.sb("den", [P, NT])
        score = ph.sb("score", [P, NT, E])
        biased = ph.sb("biased", [P, NT, E])
        best = ph.sb("best", [P, NT, 8])
        which = ph.sb("which", [P, NT, 8], U32)
        whichf = ph.sb("whichf", [P, NT, 8])
        lane = ph.sb("lane", [P, E])
        hot = ph.sb("hot", [P, 2, NT, E])
        both = ph.sb("both", [P, NT, E])
        tmp = ph.sb("tmp", [P, 2, NT, E])
        before = ph.sb("before", [P, P])
        ones = ph.sb("ones", [P, NT])
        onesq = ph.sb("onesq", [P, P])
        total = ph.sb("total", [P, NT, E])
        upto = ph.sb("upto", [P, E, NT])
        at = ph.sb("at", [P, NT, E])
        cnt = ph.sb("cnt", [P, E])
        cnti = ph.sb("cnti", [P, E], I32)
        shr = ph.sb("shr", [P, E], I32)
        padded = ph.sb("padded", [P, E])
        ends = ph.sb("ends", [P, E])
        base = ph.sb("base", [P, E])
        slotf = ph.sb("slotf", [P, 2, NT])
        chunk0 = ph.sb("chunk0", [1, ROUTED])
        past = ph.sb("past", [1, ROUTED, E])
        eidf = ph.sb("eidf", [1, NEC])
        psp = ph.ps("psp", [P, NT, E])
        pst = ph.ps("pst", [P, NT, E])
        psl = ph.ps("psl", [P, NT, E])
        made, zeroed, loaded = ph.sem("made"), ph.sem("zeroed"), ph.sem("loaded")
        by_token = ph.sem("logits_by_token")
        step, exped, counted = ph.sem("vector_steps"), ph.sem("exp_done"), ph.sem("counted")
        shift = CH.bit_length() - 1

        with nc.Block() as block:
            @block.sync
            def _(sp):
                sp.dma_start(gb[:], bcast(gate_b, 0, [P, E])).then_inc(loaded, 16)

            @block.gpsimd
            def _(pool):
                nc.gpsimd.memset(ones[:], 1.0).then_inc(made, 1)
                nc.gpsimd.memset(onesq[:], 1.0).then_inc(zeroed, 1)
                nc.gpsimd.iota(lane[:], pattern=[[1, E]], base=0, channel_multiplier=0,
                               allow_small_or_imprecise_dtypes=True).then_inc(made, 1)
                nc.gpsimd.iota(chunk0[:], pattern=[[CH, ROUTED]], base=0, channel_multiplier=0,
                               allow_small_or_imprecise_dtypes=True).then_inc(made, 1)
                pool.wait_ge(zeroed, 1)
                nc.gpsimd.affine_select(out=before[:], in_=onesq[:], compare_op=ALU.is_gt, fill=0.0,
                                        base=0, pattern=[[1, P]], channel_multiplier=-1).then_inc(made, 1)

            @block.scalar
            def _(act):
                act.wait_ge(step, 2)
                nc.scalar.activation(ex[:], ex[:], ACT.Exp).then_inc(exped, 1)

            @block.tensor
            def _(pe):
                for t in range(NT):
                    last = nc.tensor.transpose(psl[:, t], logits[:, t * P:(t + 1) * P], ident[0:E, 0:E])
                last.then_inc(by_token, 1)
                pe.wait_ge(made, 4)
                pe.wait_ge(step, BOTH_STEP)
                nc.tensor.matmul(psp[:].rearrange("p t e -> p (t e)"), before[:],
                                 both[:].rearrange("p t e -> p (t e)"), start=True, stop=True).then_inc(counted, 1)
                nc.tensor.matmul(pst[:].rearrange("p t e -> p (t e)"), onesq[:],
                                 both[:].rearrange("p t e -> p (t e)"), start=True, stop=True).then_inc(counted, 1)

            @block.vector
            def _(dve):
                V = nc.vector
                did = [0]

                def then(ins):
                    ins.then_inc(step, 1)
                    did[0] += 1
                    dve.wait_ge(step, did[0])

                wide = [P, NT, E]
                dve.wait_ge(by_token, 1)
                then(V.tensor_reduce(top[:], psl[:], AX_X, ALU.max))
                then(V.tensor_tensor(ex[:], psl[:], top[:].unsqueeze(2).broadcast_to(wide), ALU.subtract))
                dve.wait_ge(exped, 1)
                then(V.tensor_reduce(den[:], ex[:], AX_X, ALU.add))
                then(V.reciprocal(top[:], den[:]))
                then(V.tensor_tensor(score[:], ex[:], top[:].unsqueeze(2).broadcast_to(wide), ALU.mult))
                dve.wait_ge(loaded, 16)
                then(V.tensor_tensor(biased[:], score[:], bcast(gb[:], 1, wide), ALU.add))
                for t in range(NT):
                    last = V.max(best[:, t], biased[:, t])
                then(last)
                for t in range(NT):
                    last = V.max_index(which[:, t], best[:, t], biased[:, t])
                then(last)
                then(V.tensor_copy(whichf[:], which[:]))
                dve.wait_ge(made, 4)
                for r in range(2):
                    then(V.tensor_tensor(hot[:, r], whichf[:, :, r:r + 1].broadcast_to(wide), bcast(lane[:], 1, wide),
                                         ALU.is_equal))
                then(V.tensor_tensor(both[:], hot[:, 0], hot[:, 1], ALU.add))
                assert did[0] == BOTH_STEP
                for r in range(2):
                    then(V.tensor_tensor(tmp[:, r], hot[:, r], score[:], ALU.mult))
                then(V.tensor_reduce(weight[:], tmp[:], AX_X, ALU.add))
                dve.wait_ge(counted, 2)
                then(V.tensor_copy(total[:], pst[:]))
                for e in range(E):
                    then(V.tensor_tensor_scan(upto[:, e], ones[:], total[:, :, e], 0.0, ALU.mult, ALU.add))
                then(V.tensor_tensor(at[:], upto[:].rearrange("p e t -> p t e"), total[:], ALU.subtract))
                then(V.tensor_tensor(at[:], at[:], psp[:], ALU.add))
                then(V.tensor_scalar(cnt[:], upto[:, :, NT - 1], float(CH - 1), None, ALU.add))
                then(V.tensor_copy(cnti[:], cnt[:]))
                then(V.tensor_scalar(shr[:], cnti[:], shift, shift, ALU.logical_shift_right,
                                     ALU.logical_shift_left))
                then(V.tensor_copy(padded[:], shr[:]))
                then(V.tensor_tensor_scan(ends[:], ones[:, 0:E], padded[:], 0.0, ALU.mult, ALU.add))
                then(V.tensor_tensor(base[:], ends[:], padded[:], ALU.subtract))
                then(V.tensor_scalar(base[:], base[:], float(NCH * CH), None, ALU.add))
                then(V.tensor_tensor(at[:], at[:], bcast(base[:], 1, wide), ALU.add))
                for r in range(2):
                    then(V.tensor_tensor(tmp[:, r], hot[:, r], at[:], ALU.mult))
                then(V.tensor_reduce(slotf[:], tmp[:], AX_X, ALU.add))
                then(V.tensor_copy(slot[:], slotf[:]))
                then(V.tensor_tensor(past[:], chunk0[:].unsqueeze(2).broadcast_to([1, ROUTED, E]),
                                     bcast(ends[0:1, :], 1, [1, ROUTED, E]), ALU.is_ge))
                then(V.memset(eidf[:], float(E)))
                then(V.tensor_reduce(eidf[:, NCH:], past[:], AX_X, ALU.add))
                then(V.tensor_scalar(eidf[:, NCH:], eidf[:, NCH:], float(E - 1), None, ALU.min))
                then(V.tensor_copy(expert_of[:], eidf[:]))


BOTH_STEP = 12


def experts(nc, ident, rin_ch, rows_in, rout_ch, w_scr, slot, expert_of):
    with ExitStack() as ctx:
        ph = Phase(nc, ctx, "moe")
        wraw = ph.sb2("wraw", [P, WROW])
        w = [[ph.sb(f"w{s}_{h}", [P, WM], F32R) for h in ("hi", "lo")] for s in range(2)]
        xin = ph.sb2("xin", [P, TPC, D])
        xt = [[ph.sb(f"xt{s}_{h}", [P, KT, CH], F32R) for h in ("hi", "lo")] for s in range(2)]
        h3 = ph.sb2("h3", [P, CH])
        u = ph.sb("u", [P, FB, CH])
        sig = ph.sb("sig", [P, KT, CH])
        a = ph.sb("a", [P, KT, CH])
        ah = [[ph.sb(f"a{s}_{h}", [P, KT, CH], F32R) for h in ("hi", "lo")] for s in range(2)]
        y = ph.sb2("y", [P, TPC, D])
        wb = ph.sb2("wb", [P, 2 * FB + D])
        sin = ph.sb2("sin", [P, TPC, D])
        sidx = ph.sb2("sidx", [P, 2, TPC], I32)
        psT = ph.ps("psT", [P, KT, CH])
        ps1 = [ph.ps(f"ps1_{i}", [P, CH]) for i in range(2)]
        ps3 = [ph.ps(f"ps3_{i}", [P, CH]) for i in range(2)]
        psY = [ph.ps(f"psY{i}", [P, 2, D]) for i in range(2)]
        w_loaded, x_loaded = ph.sem2("weights_loaded"), ph.sem2("rows_loaded")
        w_hi, w_lo, w_bias = (ph.sem2(n) for n in ("weights_hi", "weights_lo", "biases_copied"))
        turned, x_hi, x_lo = ph.sem2("rows_turned"), ph.sem2("rows_hi"), ph.sem2("rows_lo")
        p1, p3 = ph.sem2("h1_product"), ph.sem2("h3_product")
        h3_done, u_done = ph.sem2("h3_done"), ph.sem2("u_done")
        g_cut, l_cut, sig_done, gs_done, a_done = (ph.sem2(n) for n in
                                                  ("gate_cut", "linear_cut", "sigmoid_done", "gate_done", "a_done"))
        a_hi, a_lo = ph.sem2("a_hi"), ph.sem2("a_lo")
        y_done, y_biased, y_stored = ph.sem2("y_product"), ph.sem2("y_biased"), ph.sem2("y_stored")
        s_loaded, s_index, scattered = ph.sem2("tokens_loaded"), ph.sem2("index_copied"), ph.sem2("tokens_scattered")

        def wk(half, which, k):
            return half[:, (which * KT + k) * 2 * F:(which * KT + k + 1) * 2 * F]

        s_ready = ph.sem("scatter_may_start")

        with nc.Block() as block:
            @block.gpsimd
            def _(pool):
                def round_(it):
                    for s in range(2):
                        pool.wait_ge(scattered[s], it * 2 * TPC * 16)
                        pool.dma_start(sin[s][:], rin_ch[chunk_of(it, s)].rearrange("a p j d -> p (a j) d"))\
                            .then_inc(s_loaded[s], 16)
                        nc.gpsimd.tensor_copy(sidx[s][:], slot[:, :, bass.ds(it * (2 * TPC) + s * TPC, TPC)])\
                            .then_inc(s_index[s], 1)
                        pool.wait_ge(s_loaded[s], it * 16 + 16)
                        pool.wait_ge(s_index[s], it + 1)
                        pool.sem_inc(s_ready, 1)
                        for r in range(2):
                            for j in range(TPC):
                                pool.indirect_dma_start(
                                    out=rows_in, out_offset=bass.IndirectOffsetOnAxis(sidx[s][:, r, j:j + 1], 0),
                                    in_=sin[s][:, j, :], in_offset=None).then_inc(scattered[s], 16)

                in_rounds(pool, NCH // 2, round_)
                for s in range(2):
                    pool.wait_ge(scattered[s], NCH // 2 * 2 * TPC * 16)

            @block.sync
            def _(sp):
                def load(n, s):
                    sp.wait_ge(turned[s], n)
                    sp.dma_start(xin[s][:], rin_ch[chunk_of(n, s)].rearrange("a p j d -> p (a j) d"))\
                        .then_inc(x_loaded[s], 16)
                    sp.wait_ge(w_lo[s], n * 2)
                    sp.wait_ge(w_bias[s], n)
                    e = sp.value_load(expert_of[0:1, chunk_of(n, s)], min_val=0, max_val=E)
                    sp.dma_start(wraw[s][:], w_scr[bass.ds(e, 1)].rearrange("a p w -> (a p) w"))\
                        .then_inc(w_loaded[s], 16)

                in_rounds(sp, NCH // 2, lambda it: [load(it, s) for s in range(2)])
                for s in range(2):
                    sp.wait_ge(scattered[s], NCH // 2 * 2 * TPC * 16)
                with sp.Fori(NCH // 2, NEC // 2) as it:
                    for s in range(2):
                        load(it, s)

            @block.tensor
            def _(pe):
                def turn(n, s):
                    pe.wait_ge(x_loaded[s], n * 16 + 16)
                    if s == 1:
                        pe.wait_ge(x_lo[0], n + 1)
                    else:
                        pe.wait_ge(x_lo[1], n)
                    transposes(nc, psT, xin[s], ident).then_inc(turned[s], 1)

                def hidden(n, s, blocks):
                    pe.wait_ge(x_lo[s], n + 1)
                    pe.wait_ge(w_lo[s], n * 2 + 1)
                    for f in blocks:
                        for which, psum, done in ((1, ps3, p3), (0, ps1, p1)):
                            reader = h3_done if which else u_done
                            if f >= 2:
                                pe.wait_ge(reader[s], n * FB + f - 1)
                            elif s == 1:
                                pe.wait_ge(reader[0], n * FB + f + 3)
                            else:
                                pe.wait_ge(reader[1], n * FB)
                            i = 0
                            for k in range(KT):
                                for aa, bb in PARTS3:
                                    last = nc.tensor.matmul(psum[f % 2][:], wk(w[s][aa], which, k)[:, f * P:(f + 1) * P],
                                                            xt[s][bb][:, k], start=(i == 0), stop=(i == 5))
                                    i += 1
                            last.then_inc(done[s], 1)

                def down(n, s):
                    pe.wait_ge(a_lo[s], n + 1)
                    pe.wait_ge(w_lo[s], n * 2 + 2)
                    w2s = [w[s][i][:, W13:WM].rearrange("p (k d) -> p k d", k=KT) for i in range(2)]
                    for t in range(2):
                        if s == 1:
                            pe.wait_ge(y_biased[0], n * 2 + t + 1)
                        else:
                            pe.wait_ge(y_biased[1], n * 2)
                        for v in range(2):
                            j = 2 * t + v
                            last = product(nc, psY[t][:, v], ah[s], w2s, slice(j * P, (j + 1) * P), slice(0, D))
                        last.then_inc(y_done[s], 1)

                def step(n, s, nxt, prv):
                    if prv is None:
                        turn(0, 0)
                    if nxt is not None:
                        turn(*nxt)
                    hidden(n, s, range(0, FB - 1))
                    if prv is not None:
                        down(*prv)
                    hidden(n, s, range(FB - 1, FB))
                    if nxt is None:
                        down(n, s)

                in_pairs(pe, NEC, step)

            @block.scalar
            def _(act):
                def first_weights(n, s):
                    act.wait_ge(w_loaded[s], n * 16 + 16)
                    act.wait_ge(p1[s], n * FB)
                    nc.scalar.activation(w[s][0][:, 0:W13], wraw[s][:, 0:W13], ACT.Copy).then_inc(w_hi[s], 1)

                def rows(n, s):
                    act.wait_ge(turned[s], n + 1)
                    nc.scalar.activation(xt[s][0][:], psT[:], ACT.Copy).then_inc(x_hi[s], 1)

                def second_weights(n, s):
                    act.wait_ge(y_done[s], n * 2)
                    nc.scalar.activation(w[s][0][:, W13:], wraw[s][:, W13:WM], ACT.Copy).then_inc(w_hi[s], 1)
                    act.wait_ge(y_biased[s], n * 2)
                    nc.scalar.activation(wb[s][:], wraw[s][:, WM:], ACT.Copy).then_inc(w_bias[s], 1)

                def step(n, s, nxt, prv):
                    if prv is None:
                        first_weights(0, 0)
                        rows(0, 0)
                        second_weights(0, 0)
                    act.wait_ge(w_bias[s], n + 1)
                    for f in range(FB):
                        act.wait_ge(p3[s], n * FB + f + 1)
                        if f >= 2:
                            act.wait_ge(u_done[s], n * FB + f - 1)
                        elif s == 1:
                            act.wait_ge(u_done[0], n * FB + f + 3)
                        else:
                            act.wait_ge(u_done[1], n * FB)
                        nc.scalar.activation(h3[f % 2][:], ps3[f % 2][:], ACT.Identity,
                                             bias=wb[s][:, FB + f:FB + f + 1]).then_inc(h3_done[s], 1)
                        if f == 0 and nxt is not None:
                            first_weights(*nxt)
                        if f == 1:
                            if nxt is not None:
                                rows(*nxt)
                            act.wait_ge(g_cut[s], n + 1)
                            nc.scalar.activation(sig[:], u[:, 0:KT], ACT.Sigmoid, scale=ALPHA).then_inc(sig_done[s], 1)
                        if f == FB - 1 and nxt is not None:
                            second_weights(*nxt)
                    if prv is not None:
                        store(*prv)
                    act.wait_ge(a_done[s], n + 1)
                    act.wait_ge(y_done[s], n * 2)
                    nc.scalar.activation(ah[s][0][:], a[:], ACT.Copy).then_inc(a_hi[s], 1)
                    if nxt is None:
                        store(n, s)

                def store(n, s):
                    act.wait_ge(y_biased[s], n * 2 + 2)
                    act.dma_start(rout_ch[chunk_of(n, s)].rearrange("a p j d -> p (a j) d"), y[s][:])\
                        .then_inc(y_stored[s], 16)

                in_pairs(act, NEC, step)
                for s in range(2):
                    act.wait_ge(y_stored[s], NEC // 2 * 16)

            @block.vector
            def _(dve):
                V = nc.vector

                def first_weights(n, s):
                    dve.wait_ge(w_hi[s], n * 2 + 1)
                    V.tensor_tensor(w[s][1][:, 0:W13], wraw[s][:, 0:W13], w[s][0][:, 0:W13].bitcast(F32),
                                    ALU.subtract).then_inc(w_lo[s], 1)

                def rows(n, s):
                    dve.wait_ge(x_hi[s], n + 1)
                    V.tensor_tensor(xt[s][1][:], psT[:], xt[s][0][:].bitcast(F32), ALU.subtract).then_inc(x_lo[s], 1)

                def second_weights(n, s):
                    dve.wait_ge(w_hi[s], n * 2 + 2)
                    V.tensor_tensor(w[s][1][:, W13:], wraw[s][:, W13:WM], w[s][0][:, W13:].bitcast(F32),
                                    ALU.subtract).then_inc(w_lo[s], 1)

                def result(n, s):
                    for t in range(2):
                        dve.wait_ge(y_done[s], n * 2 + t + 1)
                        dve.wait_ge(y_stored[s], n * 16)
                        V.tensor_tensor(y[s][:, 2 * t:2 * t + 2], psY[t][:],
                                        bcast(wb[s][:, 2 * FB:], 1, [P, 2, D]), ALU.add)\
                            .then_inc(y_biased[s], 1)

                def step(n, s, nxt, prv):
                    if prv is None:
                        first_weights(0, 0)
                        rows(0, 0)
                        second_weights(0, 0)
                    dve.wait_ge(w_bias[s], n + 1)
                    for f in range(FB):
                        dve.wait_ge(h3_done[s], n * FB + f + 1)
                        dve.wait_ge(p1[s], n * FB + f + 1)
                        if f == 0 and prv is not None:
                            dve.wait_ge(a_done[prv[1]], prv[0] + 1)
                        V.scalar_tensor_tensor(u[:, f], ps1[f % 2][:], wb[s][:, f:f + 1], h3[f % 2][:],
                                               ALU.add, ALU.mult).then_inc(u_done[s], 1)
                        if f == 0 and nxt is not None:
                            first_weights(*nxt)
                        if f == KT - 1:
                            dve.wait_ge(u_done[s], n * FB + KT)
                            V.tensor_scalar(u[:, 0:KT], u[:, 0:KT], LIMIT, None, ALU.min).then_inc(g_cut[s], 1)
                            if nxt is not None:
                                rows(*nxt)
                            dve.wait_ge(sig_done[s], n + 1)
                            V.tensor_tensor(sig[:], sig[:], u[:, 0:KT], ALU.mult).then_inc(gs_done[s], 1)
                        if f == KT and prv is not None:
                            result(*prv)
                    dve.wait_ge(u_done[s], n * FB + FB)
                    V.tensor_scalar(u[:, KT:], u[:, KT:], LIMIT, -LIMIT, ALU.min, ALU.max).then_inc(l_cut[s], 1)
                    dve.wait_ge(gs_done[s], n + 1)
                    dve.wait_ge(l_cut[s], n + 1)
                    V.scalar_tensor_tensor(a[:], u[:, KT:], 1.0, sig[:], ALU.add, ALU.mult).then_inc(a_done[s], 1)
                    if nxt is not None:
                        second_weights(*nxt)
                    dve.wait_ge(a_hi[s], n + 1)
                    V.tensor_tensor(ah[s][1][:], a[:], ah[s][0][:].bitcast(F32), ALU.subtract).then_inc(a_lo[s], 1)
                    if nxt is None:
                        result(n, s)

                in_pairs(dve, NEC, step)


def combine(nc, power, rout_ch, rows_out, x1_scr, weight, slot, out_ch):
    with ExitStack() as ctx:
        ph = Phase(nc, ctx, "comb")
        sh = ph.sb2("shared", [P, TPC, D])
        x1 = ph.sb2("x1", [P, TPC, D])
        yy = ph.sb2("yy", [P, 2, TPC, D])
        acc = ph.sb2("acc", [P, TPC, D])
        res = ph.sb2("res", [P, TPC, D])
        sidx = ph.sb2("sidx", [P, 2, TPC], I32)
        wgt = ph.sb2("wgt", [P, 2, TPC])
        stats = ph.sb2("stats", [P, TPC, 6])
        mv = ph.sb2("mv", [P, TPC, 2])
        std = ph.sb2("std", [P, TPC])
        rstd = ph.sb2("rstd", [P, TPC])
        loaded, gathered, copied = ph.sem2("loaded"), ph.sem2("gathered"), ph.sem2("index_copied")
        w_copied = ph.sem2("weights_copied")
        first, second = ph.sem2("first_added"), ph.sem2("second_added")
        stats_done, mv_done = ph.sem2("stats_done"), ph.sem2("mv_done")
        stats_seen, mv_seen = ph.sem("stats_seen"), ph.sem("mv_seen")
        std_done, rstd_done, normed = ph.sem2("std_done"), ph.sem2("rstd_done"), ph.sem2("normed")
        done, stored = ph.sem2("done"), ph.sem2("stored")
        ready = ph.sem("gather_may_start")

        with nc.Block() as block:
            @block.gpsimd
            def _(pool):
                def gather(n, s):
                    pool.wait_ge(second[s], n * TPC)
                    nc.gpsimd.tensor_copy(sidx[s][:], slot[:, :, bass.ds(n * (2 * TPC) + s * TPC, TPC)])\
                        .then_inc(copied[s], 1)
                    pool.wait_ge(copied[s], n + 1)
                    pool.sem_inc(ready, 1)
                    for r in range(2):
                        for j in range(TPC):
                            pool.indirect_dma_start(
                                out=yy[s][:, r, j, :], out_offset=None, in_=rows_out,
                                in_offset=bass.IndirectOffsetOnAxis(sidx[s][:, r, j:j + 1], 0))\
                                .then_inc(gathered[s], 16)

                def step(n, s, nxt, prv):
                    if prv is None:
                        gather(0, 0)
                    if nxt is not None:
                        gather(*nxt)
                    inverse_roots(nc, pool, power, s, mv, std, rstd, mv_done, mv_seen, std_done, rstd_done, n)

                in_pairs(pool, NCH, step)

            @block.sync
            def _(sp):
                def load(n, s):
                    sp.wait_ge(done[s], n)
                    sp.dma_start(sh[s][:], rout_ch[chunk_of(n, s)].rearrange("a p j d -> p (a j) d"))\
                        .then_inc(loaded[s], 16)
                    sp.dma_start(x1[s][:], x1_scr[chunk_of(n, s)].rearrange("a p j d -> p (a j) d"))\
                        .then_inc(loaded[s], 16)

                def step(n, s, nxt, prv):
                    if prv is None:
                        load(0, 0)
                    if nxt is not None:
                        load(*nxt)
                    sp.wait_ge(done[s], n + 1)
                    sp.dma_start(out_ch[chunk_of(n, s)].rearrange("a p j d -> p (a j) d"), res[s][:])\
                        .then_inc(stored[s], 16)

                in_pairs(sp, NCH, step)
                for s in range(2):
                    sp.wait_ge(stored[s], NCH // 2 * 16)

            @block.vector
            def _(dve):
                V = nc.vector

                def step(n, s, nxt, prv):
                    V.tensor_copy(wgt[s][:], weight[:, :, bass.ds(n * (2 * TPC) + s * TPC, TPC)])\
                        .then_inc(w_copied[s], 1)
                    dve.wait_ge(w_copied[s], n + 1)
                    dve.wait_ge(loaded[s], n * 32 + 32)
                    dve.wait_ge(gathered[s], (n + 1) * 2 * TPC * 16)
                    for j in range(TPC):
                        V.scalar_tensor_tensor(acc[s][:, j], yy[s][:, 0, j], wgt[s][:, 0, j:j + 1], sh[s][:, j],
                                               ALU.mult, ALU.add).then_inc(first[s], 1)
                    for j in range(TPC):
                        dve.wait_ge(first[s], n * TPC + j + 1)
                        V.scalar_tensor_tensor(acc[s][:, j], yy[s][:, 1, j], wgt[s][:, 1, j:j + 1], acc[s][:, j],
                                               ALU.mult, ALU.add).then_inc(second[s], 1)
                    dve.wait_ge(second[s], n * TPC + TPC)
                    stats_of(nc, dve, acc[s], stats[s], mv[s], n, s, stats_done, stats_seen, mv_done)
                    dve.wait_ge(rstd_done[s], n + 1)
                    for j in range(TPC):
                        V.tensor_scalar(acc[s][:, j], acc[s][:, j], mv[s][:, j, 0:1], rstd[s][:, j:j + 1],
                                        ALU.subtract, ALU.mult).then_inc(normed[s], 1)
                    dve.wait_ge(normed[s], (n + 1) * TPC)
                    dve.wait_ge(stored[s], n * 16)
                    V.tensor_tensor(res[s][:], acc[s][:], x1[s][:], ALU.add).then_inc(done[s], 1)

                in_pairs(dve, NCH, step)


_INS = ("L0_attn_x", "L0_attn_w_q", "L0_attn_w_k", "L0_attn_w_v", "L0_attn_w_o", "L0_attn_b_o",
        "L0_ffn_gate_w", "L0_ffn_gate_b", "L0_ffn_w1", "L0_ffn_b1", "L0_ffn_w3", "L0_ffn_b3",
        "L0_ffn_w2", "L0_ffn_b2", "L0_ffn_sw1", "L0_ffn_sb1", "L0_ffn_sw3", "L0_ffn_sb3",
        "L0_ffn_sw2", "L0_ffn_sb2")


def kernel(**inputs):
    import concourse.bacc as bacc
    from concourse.bass_utils import run_bass_kernel_spmd

    nc = bacc.Bacc("TRN2", target_bir_lowering=False, num_devices=1)
    arrays, args = {}, []
    for name in _INS:
        a = np.ascontiguousarray(inputs[name])
        arrays[name] = a
        args.append(nc.dram_tensor(name, a.shape, mybir.dt.from_np(a.dtype), kind="ExternalInput").ap())
    args.append(nc.dram_tensor("out", (B, SEQ, D), F32, kind="ExternalOutput").ap())
    build(nc, *args)
    r = run_bass_kernel_spmd(nc, [arrays], core_ids=[0])
    return r.results[0]["out"]
```
